# Optimizing a Trainium2 kernel written in Bass

```python
import numpy as np
import jax
import jax.numpy as jnp

def _softmax(x, axis=-1):
    return jax.nn.softmax(x, axis=axis)

def _gelu(x):
    return jax.nn.gelu(x, approximate=True)

def _silu(x):
    return jax.nn.silu(x)

def _sigmoid(x):
    return jax.nn.sigmoid(x)

def _layernorm(x, axis=-1, eps=1e-05):
    m = jnp.mean(x, axis=axis, keepdims=True)
    v = jnp.var(x, axis=axis, keepdims=True)
    return (x - m) / jnp.sqrt(v + eps)

def _scatter_add(tgt, idx, src, axis=0):
    return tgt.at[idx].add(src)

def _segment_sum(src, seg, n):
    return jax.ops.segment_sum(src, seg, n)
kernel_name = 'mk_flamingo_gated_d1_seqx_r4_4848b8'

def setup_inputs(seed: int=0):
    np.random.seed(seed)
    _w = jnp.asarray

    def _rec_inputs():
        import jax
        import jax.numpy as jnp
        _rk = jax.random.key(seed)
        x = -0.0003929 + 0.9999 * jax.random.normal(jax.random.fold_in(_rk, 1), (16, 112, 512), jnp.float32)
        _lenS = 112 - jax.random.randint(jax.random.fold_in(_rk, 7), (16,), 0, max(1, 112 // 4) + 1, jnp.int32)
        _lenS2 = 375 - jax.random.randint(jax.random.fold_in(_rk, 8), (16,), 0, max(1, 375 // 4) + 1, jnp.int32)
        _ctx_2048P = jax.random.normal(jax.random.fold_in(_rk, 11), (16, 16, 512), jnp.float32)
        _ctx_2048c = jax.random.dirichlet(jax.random.fold_in(_rk, 511), 0.3 * jnp.ones((16,), jnp.float32), (16, 375))
        _ctx_2048t = jnp.einsum('bsk,bkd->bsd', _ctx_2048c, _ctx_2048P)
        _ctx_2048t = _ctx_2048t * jax.lax.rsqrt(jnp.mean(jnp.square(_ctx_2048t)) + 1e-12) * 0.953939
        ctx_2048 = -0.000514642 + 1.00011 * (_ctx_2048t + 0.3 * jax.random.normal(jax.random.fold_in(_rk, 611), (16, 375, 512), jnp.float32))
        _validS = jnp.arange(112)[None, :] < _lenS[:, None]
        _validS2 = jnp.arange(375)[None, :] < _lenS2[:, None]
        _causal = jnp.tril(jnp.ones((112, 112), dtype=bool))
        mask_BxS2_ik0 = jnp.where(jnp.broadcast_to(_validS2[:, :], (16, 375)), 0, 1).astype(jnp.int32)
        _g = jax.random.normal(jax.random.fold_in(_rk, 9001), (2, 1), jnp.float32)
        _g = jnp.sign(_g) * jnp.maximum(jnp.abs(_g), 1.0) + (_g == 0) * 1.0
        g_xattn = _g[0]
        g_ffn = _g[1]
        return (x, ctx_2048, mask_BxS2_ik0, g_xattn, g_ffn)
    x, ctx_2048, mask_BxS2_ik0, g_xattn, g_ffn = _rec_inputs()

    def _L0_xattn_setup():
        import jax, jax.numpy as jnp
        import numpy as np
        import math
        H = 512
        NH = 16
        HD = H // NH
        EPS_LN = 1e-05
        RES_SCALE_MAX = 0.3

        def _nan_clean(x, lim=10000.0):
            return jnp.nan_to_num(x, nan=0.0, posinf=lim, neginf=-lim)
        key = jax.random.key(seed)
        ks = jax.random.split(key, 12)
        B, S, T = (4, 512, 64)
        std = 1.0 / math.sqrt(H)
        return {'hidden_states': jax.random.normal(ks[0], (B, S, H), jnp.float32), 'audio_tokens': jax.random.normal(ks[1], (B, T, H), jnp.float32), 'attention_mask': jax.random.randint(ks[2], (B, T), 0, 2, jnp.int32), 'Wq': jax.random.normal(ks[3], (H, H), jnp.float32) * std, 'bq': jnp.zeros((H,), jnp.float32), 'Wk': jax.random.normal(ks[4], (H, H), jnp.float32) * std, 'bk': jnp.zeros((H,), jnp.float32), 'Wv': jax.random.normal(ks[5], (H, H), jnp.float32) * std, 'bv': jnp.zeros((H,), jnp.float32), 'Wo': jax.random.normal(ks[6], (H, H), jnp.float32) * std, 'bo': jnp.zeros((H,), jnp.float32), 'ln_gamma': jnp.ones((H,), jnp.float32), 'ln_beta': jnp.zeros((H,), jnp.float32), 'residual_scale': jnp.float32(0.05)}
    _L0_xattn_all = _L0_xattn_setup()
    _L0_xattn_in = {k: v for k, v in _L0_xattn_all.items() if k in ('Wq', 'bq', 'Wk', 'bk', 'Wv', 'bv', 'Wo', 'bo', 'ln_gamma', 'ln_beta', 'residual_scale')}
    del _L0_xattn_all

    def _L0_ffn_setup():
        import jax, jax.numpy as jnp
        import numpy as np
        HIDDEN = 512
        INTER = 1376
        LUT_SIZE = 16

        def _ghost_linear(x, idx, lut):
            w = lut[idx]
            return jnp.einsum('bsh,oh->bso', x, w)
        key = jax.random.key(seed)
        k_x, k_lut, k_g, k_u, k_d = jax.random.split(key, 5)
        x = jax.random.normal(k_x, (2, 1024, HIDDEN), dtype=jnp.float32)
        lut = jax.random.normal(k_lut, (LUT_SIZE,), dtype=jnp.float32) * 0.02
        gate_idx = jax.random.randint(k_g, (INTER, HIDDEN), 0, LUT_SIZE, dtype=jnp.int32)
        up_idx = jax.random.randint(k_u, (INTER, HIDDEN), 0, LUT_SIZE, dtype=jnp.int32)
        down_idx = jax.random.randint(k_d, (HIDDEN, INTER), 0, LUT_SIZE, dtype=jnp.int32)
        return {'x': x, 'lut': lut, 'gate_idx': gate_idx, 'up_idx': up_idx, 'down_idx': down_idx}
    _L0_ffn_all = _L0_ffn_setup()
    _L0_ffn_in = {k: v for k, v in _L0_ffn_all.items() if k in ('lut', 'gate_idx', 'up_idx', 'down_idx')}
    del _L0_ffn_all
    return {'x': x, 'ctx_2048': ctx_2048, 'mask_BxS2_ik0': mask_BxS2_ik0, 'g_xattn': g_xattn, 'g_ffn': g_ffn, 'L0_xattn_Wq': _L0_xattn_in['Wq'], 'L0_xattn_bq': _L0_xattn_in['bq'], 'L0_xattn_Wk': _L0_xattn_in['Wk'], 'L0_xattn_bk': _L0_xattn_in['bk'], 'L0_xattn_Wv': _L0_xattn_in['Wv'], 'L0_xattn_bv': _L0_xattn_in['bv'], 'L0_xattn_Wo': _L0_xattn_in['Wo'], 'L0_xattn_bo': _L0_xattn_in['bo'], 'L0_xattn_ln_gamma': _L0_xattn_in['ln_gamma'], 'L0_xattn_ln_beta': _L0_xattn_in['ln_beta'], 'L0_xattn_residual_scale': _L0_xattn_in['residual_scale'], 'L0_ffn_lut': _L0_ffn_in['lut'], 'L0_ffn_gate_idx': _L0_ffn_in['gate_idx'], 'L0_ffn_up_idx': _L0_ffn_in['up_idx'], 'L0_ffn_down_idx': _L0_ffn_in['down_idx']}

def reference(x, ctx_2048, mask_BxS2_ik0, g_xattn, g_ffn, L0_xattn_Wq, L0_xattn_bq, L0_xattn_Wk, L0_xattn_bk, L0_xattn_Wv, L0_xattn_bv, L0_xattn_Wo, L0_xattn_bo, L0_xattn_ln_gamma, L0_xattn_ln_beta, L0_xattn_residual_scale, L0_ffn_lut, L0_ffn_gate_idx, L0_ffn_up_idx, L0_ffn_down_idx):
    import jax
    import jax.numpy as jnp

    def _L0_xattn_ref(hidden_states, audio_tokens, attention_mask, Wq, bq, Wk, bk, Wv, bv, Wo, bo, ln_gamma, ln_beta, residual_scale):
        import jax, jax.numpy as jnp
        import numpy as np
        import math
        H = 512
        NH = 16
        HD = H // NH
        EPS_LN = 1e-05
        RES_SCALE_MAX = 0.3

        def _nan_clean(x, lim=10000.0):
            return jnp.nan_to_num(x, nan=0.0, posinf=lim, neginf=-lim)
        B, S, _ = hidden_states.shape
        T = audio_tokens.shape[1]
        hs = _nan_clean(hidden_states).astype(jnp.float32)
        at = _nan_clean(audio_tokens).astype(jnp.float32)

        def proj(x, W, b, L):
            y = x @ W.T + b
            return y.reshape(B, L, NH, HD).transpose(0, 2, 1, 3)
        q = _nan_clean(proj(hs, Wq, bq, S))
        k = _nan_clean(proj(at, Wk, bk, T))
        v = _nan_clean(proj(at, Wv, bv, T))
        scale = max(math.sqrt(HD), 1e-08)
        scores = jnp.einsum('bhsd,bhtd->bhst', q, k) / scale
        scores = jnp.clip(scores, -50.0, 50.0)
        scores = jnp.nan_to_num(scores, nan=0.0, posinf=50.0, neginf=-50.0)
        attend = (attention_mask.astype(jnp.float32) > 0.5)[:, None, None, :]
        scores = jnp.where(attend, scores, -10000.0)
        scores = jnp.clip(scores, -50.0, 50.0)
        probs = jax.nn.softmax(scores, axis=-1)
        probs = jnp.nan_to_num(probs, nan=0.0, posinf=1.0, neginf=0.0)
        probs = probs / (probs.sum(axis=-1, keepdims=True) + 1e-08)
        ctx = jnp.einsum('bhst,bhtd->bhsd', probs, v)
        ctx = ctx.transpose(0, 2, 1, 3).reshape(B, S, H)
        delta = _nan_clean(ctx @ Wo.T + bo)
        rs = jnp.clip(residual_scale, 0.0, RES_SCALE_MAX)
        delta = rs * delta
        mu = delta.mean(axis=-1, keepdims=True)
        var = jnp.mean((delta - mu) ** 2, axis=-1, keepdims=True)
        delta = (delta - mu) / jnp.sqrt(var + EPS_LN) * ln_gamma + ln_beta
        return delta

    def _L0_ffn_ref(x, lut, gate_idx, up_idx, down_idx):
        import jax, jax.numpy as jnp
        import numpy as np
        HIDDEN = 512
        INTER = 1376
        LUT_SIZE = 16

        def _ghost_linear(x, idx, lut):
            w = lut[idx]
            return jnp.einsum('bsh,oh->bso', x, w)
        gate = _ghost_linear(x, gate_idx, lut)
        up = _ghost_linear(x, up_idx, lut)
        h = jax.nn.silu(gate) * up
        return _ghost_linear(h, down_idx, lut)
    x = x + jnp.tanh(g_xattn[0]) * _L0_xattn_ref(_layernorm(x, axis=-1), ctx_2048, mask_BxS2_ik0, L0_xattn_Wq, L0_xattn_bq, L0_xattn_Wk, L0_xattn_bk, L0_xattn_Wv, L0_xattn_bv, L0_xattn_Wo, L0_xattn_bo, L0_xattn_ln_gamma, L0_xattn_ln_beta, L0_xattn_residual_scale)
    x = x + jnp.tanh(g_ffn[0]) * _L0_ffn_ref(_layernorm(x, axis=-1), L0_ffn_lut, L0_ffn_gate_idx, L0_ffn_up_idx, L0_ffn_down_idx)
    return x

_drawn_inputs = setup_inputs


def setup_inputs(seed=0):
    import zlib

    import numpy as np

    out = dict(_drawn_inputs(seed))
    spreads = {'L0_xattn_bq': (0.0, 0.309),
     'L0_xattn_bk': (0.0, 0.8),
     'L0_xattn_bv': (0.0, 0.1),
     'L0_xattn_bo': (0.0, 0.1),
     'L0_xattn_ln_gamma': (1.0, 0.2),
     'L0_xattn_ln_beta': (0.0, 0.1)}
    factors = {}
    for name, (base, spread) in spreads.items():
        noise = np.random.default_rng([zlib.crc32(name.encode()), seed]).standard_normal(out[name].shape)
        drawn = base * np.exp(spread * noise) if base else spread * noise
        out[name] = jnp.asarray(drawn.astype(out[name].dtype))
    for name, factor in factors.items():
        out[name] = (out[name] * factor).astype(out[name].dtype)
    return out
```

```python
from contextlib import ExitStack

import concourse.bass as bass
from concourse import mybir

B, S, T, H, NH = 16, 112, 375, 512, 16
INTER = 1376
P = 128
HD = H // NH
KT = H // P
HG = P // HD
NG = NH // HG
TT = 3
TP = T // TT
TE = T + 1
ROWS = B * S
CB = 4
NC = B // CB
CH = CB * S
GC = HG * S
JT = -(-INTER // P)
JW = [min(P, INTER - j * P) for j in range(JT)]
JCOL = [j * (2 * KT * P + H) for j in range(JT)]
WCOLS = JCOL[-1] + 2 * KT * JW[-1] + H
LP = 512
LB = 2
LREST = WCOLS - B * LB * LP
LUT = 16
NPAIR = LUT // 2
MASK_BITS = 14
EPS_LN = 1e-5
EPS_PROBS = 1e-8
SCORE_SCALE = HD ** -0.5
CLIP_HI = float(2.718281828459045 ** 50.0)
CLIP_LO = float(2.718281828459045 ** -50.0)
RES_MAX = 0.3


def flamingo_kernel(nc, ins, out_t):
    fp32, fp32r, bf16 = mybir.dt.float32, mybir.dt.float32r, mybir.dt.bfloat16
    i32, u16 = mybir.dt.int32, mybir.dt.uint16
    ALU = mybir.AluOpType
    ACT = mybir.ActivationFunctionType

    def need(engine, sem, value):
        if isinstance(value, int) and value <= 0:
            return
        engine.wait_ge(sem, value)

    def need_apart(engine, sem, value):
        need(engine, sem, value)
        engine.nop(nofuse=True)

    q_dram = nc.dram_tensor("q_parts", (P, 2, NG, ROWS), fp32, kind="Internal").ap()
    w_dram = nc.dram_tensor("w_parts", (P, 2, WCOLS), fp32, kind="Internal").ap()
    xn_dram = nc.dram_tensor("xn_parts", (P, 2, KT, ROWS), fp32, kind="Internal").ap()
    x1_dram = nc.dram_tensor("x1_rows_t", (P, KT, ROWS), fp32, kind="Internal").ap()

    top = ExitStack()
    with top:
        def sb(stack, name, shape, dt=fp32):
            return stack.enter_context(nc.sbuf_tensor(name, shape, dt))

        def ps(stack, name, shape, dt=fp32):
            return stack.enter_context(nc.psum_tensor(name, shape, dt))

        def sem(name):
            return top.enter_context(nc.semaphore(name))

        work = [ps(top, f"work{i}", [P, 512]) for i in range(2)]
        score_ps = [ps(top, f"score_ps{i}", [P, 512]) for i in range(2)]
        pv_ps = [ps(top, f"pv_ps{i}", [P, 512]) for i in range(2)]
        pair_ps = [ps(top, f"pair_ps{i}", [P, 512]) for i in range(2)]

        ident = sb(top, "ident", [P, P])
        neg_half = sb(top, "neg_half", [P, CB])
        lut = sb(top, "lut", [P, LUT])
        lut_step = sb(top, "lut_step", [P, NPAIR])
        gates = sb(top, "gates", [P, 2])
        tanh_g = sb(top, "tanh_g", [P, 2])
        res = sb(top, "res", [P, 2])

        att = ExitStack()
        wk = [sb(att, f"wk{i}", [P, KT, H], fp32r) for i in range(2)]
        wv = [sb(att, f"wv{i}", [P, KT, H], fp32r) for i in range(2)]
        wo = [sb(att, f"wo{i}", [P, KT, H], fp32r) for i in range(2)]
        bq = sb(att, "bq", [P, KT])
        bk = sb(att, "bk", [P, KT])
        bv = sb(att, "bv", [P, NG])
        bo = sb(att, "bo", [P, H])
        gamma = sb(att, "gamma", [P, H])
        beta = sb(att, "beta", [P, H])
        mask = sb(att, "mask", [TP, TT, B], i32)
        prob_cap = sb(att, "prob_cap", [TP, TT, B])
        idx = sb(att, "idx", [P, LB * LP], i32)
        bit0 = sb(att, "bit0", [P, LB * LP], i32)
        pair_id = sb(att, "pair_id", [P, LB * LP], i32)
        pair_bf = sb(att, "pair_bf", [P, LP], bf16)
        pair_mask = sb(att, "pair_mask", [P, NPAIR, LP], u16)
        w_val = [sb(att, f"w_val{i}", [P, LP]) for i in range(2)]
        w_hi = sb(att, "w_hi", [P, LP], fp32r)
        w_lo = sb(att, "w_lo", [P, LP], fp32r)

        pre = ExitStack()
        stage = [sb(pre, f"stage{i}", [P, KT, H]) for i in range(2)]
        wq = [sb(pre, f"wq{i}", [P, KT, H], fp32r) for i in range(2)]
        xq = [sb(pre, f"xq{i}", [S, CB, H]) for i in range(2)]
        qstats = sb(pre, "qstats", [S, CB, 6])
        qmv = sb(pre, "qmv", [S, CB, 2])
        qvar = sb(pre, "qvar", [S, CB])
        qrstd = sb(pre, "qrstd", [S, CB])
        hs = sb(pre, "hs", [S, CB, H])
        hs_t = [sb(pre, f"hs_t{i}", [P, KT, CH], fp32r) for i in range(2)]
        q_out = sb(pre, "q_out", [P, 2, 2, CH], fp32r)

        c_const = sem("c_const")
        c_mask = sem("c_mask")
        c_w = [sem(f"c_w{i}") for i in range(2)]
        c_x = [sem(f"c_x{i}") for i in range(2)]
        c_idx = sem("c_idx")
        c_ident = sem("c_ident")
        neg_half_set = sem("neg_half_set")
        tanh_done = sem("tanh_done")
        consts_done = sem("consts_done")
        cap_done = sem("cap_done")
        wsplit_hi = sem("wsplit_hi")
        wsplit_lo = sem("wsplit_lo")
        q_stats = sem("q_stats")
        q_rstd = sem("q_rstd")
        q_pool = sem("q_pool")
        hs_done = sem("hs_done")
        hs_tr = sem("hs_tr")
        hs_hi = sem("hs_hi")
        hs_lo = sem("hs_lo")
        q_mm = sem("q_mm")
        q_hi = sem("q_hi")
        q_lo = sem("q_lo")
        q_stored = [sem(f"q_stored{i}") for i in range(2)]
        bits_done = sem("bits_done")
        masks_done = sem("masks_done")
        pair_done = sem("pair_done")
        base_done = sem("base_done")
        picked = sem("picked")
        w_hi_done = sem("w_hi_done")
        w_lo_done = sem("w_lo_done")
        w_stored = sem("w_stored")

        def lookup_bits(dve, n, k, width):
            part = slice(k * LP, k * LP + width)
            need(dve, pair_done, NPAIR * (n))
            need(dve, picked, 7 * n)
            nc.vector.tensor_scalar(bit0[:, part], idx[:, part], 1, None, ALU.bitwise_and).then_inc(bits_done, 1)
            nc.vector.tensor_scalar(pair_id[:, part], idx[:, part], MASK_BITS, None, ALU.bitwise_and).then_inc(bits_done, 1)
            dve.wait_ge(bits_done, 3 * n + 2)
            nc.vector.tensor_copy(pair_bf[:, 0:width], pair_id[:, part]).then_inc(bits_done, 1)
            dve.wait_ge(bits_done, 3 * n + 3)
            for j in range(1, NPAIR):
                nc.vector.tensor_scalar(pair_mask[:, j, 0:width], pair_bf[:, 0:width], float(2 * j), None,
                                        ALU.is_equal).then_inc(masks_done, 1)

        def lookup_pair(act, n, k, width, j):
            part = slice(k * LP, k * LP + width)
            if j == 0:
                act.wait_ge(bits_done, 3 * n + 1)
                need(act, w_lo_done, n - 1)
                nc.scalar.activation(w_val[k][:, 0:width], bit0[:, part], ACT.Identity,
                                     scale=lut_step[:, 0:1], bias=lut[:, 0:1]).then_inc(pair_done, 1)
                return
            need(act, picked, 7 * n + j - 2)
            nc.scalar.activation(pair_ps[(k * 7 + j - 1) % 2][:, 0:width], bit0[:, part], ACT.Identity,
                                 scale=lut_step[:, j:j + 1], bias=lut[:, 2 * j:2 * j + 1]).then_inc(pair_done, 1)

        def lookup_pick(dve, n, k, width, j):
            dve.wait_ge(pair_done, NPAIR * n + j + 1)
            dve.wait_ge(masks_done, 7 * n + j)
            need_apart(dve, picked, 7 * n + j - 1)
            nc.vector.copy_predicated(w_val[k][:, 0:width], pair_mask[:, j, 0:width],
                                      pair_ps[(k * 7 + j - 1) % 2][:, 0:width]).then_inc(picked, 1)

        def lookup_hi(act, n, k, width):
            act.wait_ge(picked, 7 * (n + 1))
            need(act, w_stored, 32 * n)
            nc.scalar.activation(w_hi[:, 0:width], w_val[k][:, 0:width], ACT.Copy).then_inc(w_hi_done, 1)

        def lookup_lo(pool, n, k, width):
            pool.wait_ge(w_hi_done, n + 1)
            nc.gpsimd.tensor_tensor(w_lo[:, 0:width], w_val[k][:, 0:width], w_hi[:, 0:width],
                                    ALU.subtract).then_inc(w_lo_done, 1)

        def lookup_store(sp, n, width, col):
            sp.wait_ge(w_lo_done, n + 1)
            sp.dma_start(w_dram[:, 0, bass.ds(col, width)], w_hi[:, 0:width].bitcast(fp32)).then_inc(w_stored, 16)
            sp.dma_start(w_dram[:, 1, bass.ds(col, width)], w_lo[:, 0:width].bitcast(fp32)).then_inc(w_stored, 16)

        N_CONST = 11
        with nc.Block() as block:
            @block.sync
            def _(sp):
                sp.dma_start(xq[0][:], ins["x4"][0]).then_inc(c_x[0], 16)
                sp.dma_start(stage[0][:], ins["wq"]).then_inc(c_w[0], 16)
                sp.dma_start(xq[1][:], ins["x4"][1]).then_inc(c_x[1], 16)
                for tile, name in ((bq, "bq"), (bk, "bk"), (bv, "bv"), (bo, "bo"), (gamma, "gamma"), (beta, "beta"),
                                   (lut, "lut")):
                    sp.dma_start(tile[:], ins[name]).then_inc(c_const, 16)
                sp.dma_start(gates[:, 0:1], ins["g_xattn"]).then_inc(c_const, 16)
                sp.dma_start(gates[:, 1:2], ins["g_ffn"]).then_inc(c_const, 16)
                sp.dma_start(res[:, 0:1], ins["res"]).then_inc(c_const, 16)
                sp.dma_start(mask[:], ins["mask"]).then_inc(c_const, 16)
                sp.dma_start(stage[1][:], ins["wk"]).then_inc(c_w[1], 16)
                sp.dma_start(idx[:, 0:LREST], ins["idx"][:, WCOLS - LREST:WCOLS]).then_inc(c_idx, 16)
                sp.wait_ge(wsplit_lo, 1)
                sp.dma_start(stage[0][:], ins["wv"]).then_inc(c_w[0], 16)

                def chunk(c, slot):
                    for m in range(KT):
                        sp.wait_ge(q_lo, KT * c + m + 1)
                        sp.dma_start(q_dram[:, :, m, bass.ds(c * CH, CH)], q_out[:, m % 2, :, :].bitcast(fp32)).then_inc(q_stored[m % 2], 16)
                        if m == 0:
                            if isinstance(c, int) and c + 2 < NC:
                                sp.wait_ge(hs_done, CB * (c + 1))
                                sp.dma_start(xq[slot][:], ins["x4"][c + 2]).then_inc(c_x[slot], 16)
                for c in range(NC):
                    chunk(c, c % 2)
                    if c == 0:
                        sp.wait_ge(wsplit_lo, 2)
                        sp.dma_start(stage[1][:], ins["wo"]).then_inc(c_w[1], 16)
                lookup_store(sp, 0, LREST, WCOLS - LREST)
                for i in range(2):
                    sp.wait_ge(q_stored[i], 16 * NC * KT // 2)

            @block.gpsimd
            def _(pool):
                nc.gpsimd.memset(ident[:], 0.0).then_inc(c_ident, 1)
                nc.gpsimd.memset(neg_half[:], -0.5).then_inc(neg_half_set, 1)
                pool.wait_ge(c_ident, 1)
                nc.gpsimd.affine_select(out=ident[:], in_=ident[:], compare_op=ALU.not_equal, fill=1.0, base=0,
                                        pattern=[[-1, P]], channel_multiplier=1).then_inc(c_ident, 1)
                pool.wait_ge(neg_half_set, 1)
                for c in range(NC):
                    pool.wait_ge(q_stats, 2 * CB * (c + 1))
                    nc.gpsimd.tensor_scalar(qvar[:], qmv[:, :, 1], EPS_LN, 1.0, ALU.add, ALU.mult).then_inc(q_pool, 1)
                    pool.wait_ge(q_pool, c + 1)
                    need(pool, hs_done, CB * c)
                    nc.gpsimd.tensor_tensor(qrstd[:], qvar[:], neg_half[0:S, :], ALU.pow).then_inc(q_rstd, 1)
                lookup_lo(pool, 0, 0, LREST)

            @block.scalar
            def _(act):
                def split_hi(i, dst):
                    act.wait_ge(c_w[i % 2], 16 * (i // 2 + 1))
                    nc.scalar.activation(dst[0][:], stage[i % 2][:], ACT.Copy).then_inc(wsplit_hi, 1)
                split_hi(0, wq)
                act.wait_ge(c_const, 16 * N_CONST)
                nc.scalar.activation(tanh_g[:], gates[:], ACT.Tanh).then_inc(tanh_done, 1)

                def chunk(c):
                    for k in range(KT):
                        act.wait_ge(hs_tr, KT * c + k + 1)
                        if k == 0:
                            need(act, q_mm, KT * c)
                        nc.scalar.activation(hs_t[0][:, k, :], work[k % 2][:, 0:CH], ACT.Copy).then_inc(hs_hi, 1)
                    for m in range(KT):
                        act.wait_ge(q_mm, KT * c + m + 1)
                        need(act, q_stored[m % 2], 16 * ((KT * c + m) // 2))
                        nc.scalar.activation(q_out[:, m % 2, 0, :], work[m % 2][:, 0:CH], ACT.Identity,
                                             bias=bq[:, m:m + 1]).then_inc(q_hi, 1)
                act.wait_ge(consts_done, 1)
                for c in range(NC):
                    chunk(c)
                    if c < 3:
                        split_hi(c + 1, (wk, wv, wo)[c])
                    if c == 0:
                        for j in range(NPAIR):
                            lookup_pair(act, 0, 0, LREST, j)
                    if c == 1:
                        lookup_hi(act, 0, 0, LREST)

            @block.vector
            def _(dve):
                def stats(c):
                    dve.wait_ge(c_x[c % 2], 16 * (c // 2 + 1))
                    for i in range(CB):
                        nc.vector.bn_stats(qstats[:, i, :], xq[c % 2][:, i, :]).then_inc(q_stats, 1)
                    dve.wait_ge(q_stats, 2 * CB * c + CB)
                    for i in range(CB):
                        nc.vector.bn_aggr(qmv[:, i, :], qstats[:, i, :]).then_inc(q_stats, 1)

                def normalise(c):
                    dve.wait_ge(q_rstd, c + 1)
                    need(dve, hs_tr, KT * c)
                    for i in range(CB):
                        nc.vector.tensor_scalar(hs[:, i, :], xq[c % 2][:, i, :], qmv[:, i, 0:1], qrstd[:, i:i + 1],
                                                ALU.subtract, ALU.mult).then_inc(hs_done, 1)

                def split_lo(i, dst):
                    dve.wait_ge(wsplit_hi, i + 1)
                    nc.vector.tensor_tensor(dst[1][:], stage[i % 2][:], dst[0][:], ALU.subtract).then_inc(wsplit_lo, 1)
                stats(0)
                normalise(0)
                split_lo(0, wq)
                dve.wait_ge(c_const, 16 * N_CONST)
                nc.vector.tensor_tensor(lut_step[:], lut[:, 1:LUT:2], lut[:, 0:LUT:2], ALU.subtract).then_inc(consts_done, 1)
                nc.vector.tensor_scalar(res[:, 0:1], res[:, 0:1], 0.0, RES_MAX, ALU.max, ALU.min).then_inc(cap_done, 1)
                dve.wait_ge(tanh_done, 1)
                nc.vector.tensor_scalar(gamma[:], gamma[:], tanh_g[:, 0:1], None, ALU.mult).then_inc(cap_done, 1)
                nc.vector.tensor_scalar(beta[:], beta[:], tanh_g[:, 0:1], None, ALU.mult).then_inc(cap_done, 1)
                dve.wait_ge(cap_done, 1)
                nc.vector.tensor_tensor(res[:, 1:2], res[:, 0:1], res[:, 0:1], ALU.mult).then_inc(cap_done, 1)
                nc.vector.tensor_scalar(prob_cap[:], mask[:], 0.5, CLIP_HI, ALU.is_gt, ALU.mult).then_inc(cap_done, 1)
                dve.wait_ge(cap_done, 5)
                nc.vector.tensor_scalar(prob_cap[:], prob_cap[:], CLIP_LO, None, ALU.max).then_inc(cap_done, 1)
                dve.wait_ge(c_idx, 16)
                lookup_bits(dve, 0, 0, LREST)

                def hs_low(c):
                    for k in range(KT):
                        dve.wait_ge(hs_hi, KT * c + k + 1)
                        nc.vector.tensor_tensor(hs_t[1][:, k, :], work[k % 2][:, 0:CH], hs_t[0][:, k, :],
                                                ALU.subtract).then_inc(hs_lo, 1)
                hs_low(0)
                for c in range(NC):
                    if c + 1 < NC:
                        stats(c + 1)
                        normalise(c + 1)
                    for m in range(KT):
                        dve.wait_ge(q_hi, KT * c + m + 1)
                        nc.vector.scalar_tensor_tensor(q_out[:, m % 2, 1, :], work[m % 2][:, 0:CH], bq[:, m:m + 1],
                                                       q_out[:, m % 2, 0, :], ALU.add, ALU.subtract).then_inc(q_lo, 1)
                    if c < 3:
                        split_lo(c + 1, (wk, wv, wo)[c])
                    if c == 0:
                        for j in range(1, NPAIR):
                            lookup_pick(dve, 0, 0, LREST, j)
                    if c + 1 < NC:
                        hs_low(c + 1)

            @block.tensor
            def _(pe):
                pe.wait_ge(c_ident, 2)
                for c in range(NC):
                    for k in range(KT):
                        if k == 0:
                            pe.wait_ge(hs_done, CB * (c + 1))
                            need(pe, q_lo, KT * c - 1)
                        elif k == 1:
                            need(pe, q_lo, KT * c)
                        else:
                            pe.wait_ge(hs_lo, KT * c + k - 1)
                        for i in range(CB):
                            mm = nc.tensor.transpose(work[k % 2][:, i * S:(i + 1) * S], hs[:, i, k * P:(k + 1) * P],
                                                     ident[0:S, 0:S])
                        mm.then_inc(hs_tr, 1)
                    if c == 0:
                        pe.wait_ge(wsplit_lo, 1)
                    pe.wait_ge(hs_lo, KT * (c + 1))
                    for m in range(KT):
                        need(pe, q_lo, KT * c + m - 1)
                        for n, (a, b) in enumerate([(a, b) for a, b in ((0, 0), (0, 1), (1, 0))]):
                            for k in range(KT):
                                mm = nc.tensor.matmul(work[m % 2][:, 0:CH], wq[a][:, k, m * P:(m + 1) * P],
                                                      hs_t[b][:, k, :], start=(n == 0 and k == 0),
                                                      stop=(n == 2 and k == KT - 1))
                        mm.then_inc(q_mm, 1)
        pre.close()

        ctx_in = sb(att, "ctx_in", [P, KT, T])
        ctx_t = [[sb(att, f"ctx_t{s}{i}", [P, KT, TE], fp32r) for i in range(2)] for s in range(2)]
        k_t = [[sb(att, f"k_t{s}{i}", [P, NG, TE], fp32r) for i in range(2)] for s in range(2)]
        val = [sb(att, f"val{s}", [TP, TT, NH // 2, 3, HD]) for s in range(2)]
        q_blk = sb(att, "q_blk", [P, 2, NG, GC], fp32r)
        prob = [sb(att, f"prob{s}", [TP, TT, GC]) for s in range(2)]
        den = [sb(att, f"den{s}", [P, 2, S]) for s in range(2)]
        att_t = sb(att, "att_t", [P, NG, S])
        att_p = [sb(att, f"att_p{i}", [P, NG, S], fp32r) for i in range(2)]
        xr = [sb(att, f"xr{s}", [S, H]) for s in range(2)]
        xb = sb(att, "xb", [S, H])
        delta = sb(att, "delta", [S, H])
        x1 = sb(att, "x1", [S, H])
        xn = sb(att, "xn", [S, H])
        stats_b = sb(att, "stats_b", [S, 2, 6])
        mv = sb(att, "mv", [S, 2, 2])
        rs_b = sb(att, "rs_b", [S, 6])
        xn_p = sb(att, "xn_p", [P, 2, KT, S], fp32r)
        x1_t = sb(att, "x1_t", [P, KT, S])

        ctx_loaded = sem("ctx_loaded")
        q_loaded = sem("q_loaded")
        x_loaded = [sem(f"x_loaded{i}") for i in range(2)]
        idx_loaded = sem("idx_loaded")
        zeroed = sem("zeroed")
        ctx_hi = sem("ctx_hi")
        ctx_lo = sem("ctx_lo")
        k_mm = sem("k_mm")
        k_hi = sem("k_hi")
        k_lo = sem("k_lo")
        v_mm = sem("v_mm")
        v_copied = sem("v_copied")
        scores_done = sem("scores_done")
        exp_done = sem("exp_done")
        clip_done = sem("clip_done")
        pv_done = sem("pv_done")
        den_done = sem("den_done")
        divided = sem("divided")
        att_sum = sem("att_sum")
        att_hi = sem("att_hi")
        att_lo = sem("att_lo")
        o_mm = sem("o_mm")
        ln_dve = sem("ln_dve")
        ln_pool = sem("ln_pool")
        xb_done = sem("xb_done")
        xn_tr = sem("xn_tr")
        xn_hi = sem("xn_hi")
        xn_lo = sem("xn_lo")
        x1_tr = sem("x1_tr")
        x1_copied = sem("x1_copied")
        rows_stored = sem("rows_stored")
        inverted = sem("inverted")

        def by_pair(half, row, u):
            return pv_ps[half][row:row + HD, 0:4 * S].rearrange("p (g u s) -> p g u s", g=2, u=2)[:, :, u, :]

        LN = 9
        LNP = 5

        with nc.Block() as block:
            @block.tensor
            def _(pe):
                def parts(out, left, right, n_of):
                    todo = [(a, b, k) for a, b in ((0, 0), (0, 1), (1, 0)) for k in range(KT)]
                    for n, (a, b, k) in enumerate(todo):
                        mm = nc.tensor.matmul(out, left(a, k), right(b, k), start=(n == 0), stop=(n == len(todo) - 1))
                        if n == len(todo) // 2 - 1:
                            yield mm
                    mm.then_inc(n_of, 1)
                    yield mm

                def k_unit(n, s, m):
                    if m == 0:
                        pe.wait_ge(ctx_lo, n + 1)
                        need(pe, v_copied, TT * n)
                        if isinstance(n, int) and n == 0:
                            pe.wait_ge(zeroed, 4)
                    else:
                        if m == 2:
                            need(pe, ln_dve, LN * (n - 2) + 1)
                        else:
                            pe.wait_ge(k_lo, NG * n + {1: 1, 3: 2}[m])
                    bank = work[1 if m == 2 else 0]
                    return parts(bank[:, 0:TE], lambda a, k: wk[a][:, k, m * P:(m + 1) * P],
                                 lambda b, k: ctx_t[s][b][:, k, :], k_mm)

                def v_unit(n, s, t):
                    if t == 0:
                        pe.wait_ge(k_lo, NG * n + 3)
                    elif t == 1:
                        pe.wait_ge(k_lo, NG * n + 4)
                    else:
                        pe.wait_ge(v_copied, TT * n + 2)
                    bank = work[1 if t == 0 else 0]
                    return parts(bank[0:TP, :], lambda a, k: ctx_t[s][a][:, k, t * TP:(t + 1) * TP],
                                 lambda b, k: wv[b][:, k, :], v_mm)

                def out_proj(b):
                    pe.wait_ge(att_lo, b + 1)
                    need(pe, x1_copied, b)
                    for _ in parts(work[1][0:S, :], lambda a, k: att_p[a][:, k, :], lambda c, k: wo[c][:, k, :], o_mm):
                        pass

                def transposed(src, done):
                    for k in range(KT):
                        mm = nc.tensor.transpose(work[1][:, k * S:(k + 1) * S], src[:, k * P:(k + 1) * P],
                                                 ident[0:S, 0:S])
                    mm.then_inc(done, 1)

                def scores(b, s, g, t):
                    i = TT * g + t
                    if i == 0:
                        pe.wait_ge(q_loaded, 64 * (b + 1))
                    if t == 0:
                        pe.wait_ge(k_lo, NG * b + g + 1)
                    need(pe, exp_done, TT * NG * b + i - 1)
                    for n, (a, c) in enumerate(((0, 0), (0, 1), (1, 0))):
                        mm = nc.tensor.matmul(score_ps[i % 2][0:TP, 0:GC], k_t[s][a][:, g, t * TP:(t + 1) * TP],
                                              q_blk[:, c, g, :], start=(n == 0), stop=(n == 2))
                    mm.then_inc(scores_done, 1)

                def pv(b, s, g):
                    pe.wait_ge(clip_done, TT * (NG * b + g + 1))
                    if g == 0:
                        pe.wait_ge(v_copied, TT * (b + 1))
                    if g % 2 == 0:
                        need(pe, divided, 4 * (2 * b + g // 2 - 1))
                    for u in range(2):
                        for t in range(TT):
                            for odd in range(2):
                                j = 2 * u + odd
                                h = HG * g + j
                                col = ((g % 2) * 2 + u) * S
                                mm = nc.tensor.matmul(pv_ps[g // 2][64 * odd:64 * odd + 64, col:col + S],
                                                      val[s][:, t, h // 2, odd:odd + 2, :],
                                                      prob[g % 2][:, t, j * S:(j + 1) * S],
                                                      start=(t == 0), stop=(t == TT - 1))
                    mm.then_inc(pv_done, 1)

                def iteration(b, s, attend, project, tail):
                    idle = iter(lambda: None, 0)
                    ku = vu = None
                    if project:
                        def units():
                            for m in range(NG):
                                yield from k_unit(b + 1, 1 - s, m)
                            for t in range(TT):
                                yield from v_unit(b + 1, 1 - s, t)
                        filler = units()
                    else:
                        filler = idle
                    fill = lambda: next(filler)
                    sc = (lambda g, t: scores(b, s, g, t)) if attend else (lambda g, t: None)
                    out = (lambda g: pv(b, s, g)) if attend else (lambda g: None)
                    sc(0, 0); fill(); sc(0, 1); fill(); sc(0, 2)
                    if tail:
                        out_proj(b - 1)
                    sc(1, 0); fill(); sc(1, 1); fill(); sc(1, 2)
                    out(0); fill()
                    sc(2, 0); fill(); sc(2, 1); fill(); sc(2, 2)
                    out(1); fill()
                    sc(3, 0); fill(); sc(3, 1); fill(); sc(3, 2)
                    out(2); fill()
                    if tail:
                        pe.wait_ge(ln_dve, LN * (b - 1) + 9)
                        need(pe, v_copied, TT * (b + 1) + 1 if project else 0)
                        transposed(xn, xn_tr)
                    fill()
                    out(3); fill()
                    if tail:
                        pe.wait_ge(xn_lo, b)
                        transposed(x1, x1_tr)
                    fill()

                iteration(-1, 1, False, True, False)
                iteration(0, 0, True, True, False)
                iteration(1, 1, True, True, True)
                iteration(2, 0, True, True, True)
                with pe.Fori(3, B - 2, 2) as i:
                    iteration(i, 1, True, True, True)
                    iteration(i + 1, 0, True, True, True)
                iteration(B - 1, 1, True, False, True)
                iteration(B, 0, False, False, True)

            @block.scalar
            def _(act):
                def split_ctx(n, s):
                    act.wait_ge(ctx_loaded, 16 * (n + 1))
                    need(act, v_mm, TT * (n - 1))
                    nc.scalar.activation(ctx_t[s][0][:, :, 0:T], ctx_in[:], ACT.Copy).then_inc(ctx_hi, 1)

                def key_hi(n, s, m):
                    act.wait_ge(k_mm, NG * n + m + 1)
                    if m == 0:
                        need(act, scores_done, TT * NG * (n - 1))
                    nc.scalar.activation(k_t[s][0][:, m, :], work[1 if m == 2 else 0][:, 0:TE], ACT.Identity,
                                         bias=bk[:, m:m + 1]).then_inc(k_hi, 1)

                def value(n, s, t):
                    act.wait_ge(v_mm, TT * n + t + 1)
                    if t == 0:
                        need(act, pv_done, NG * (n - 1))
                        if isinstance(n, int) and n < 2:
                            act.wait_ge(zeroed, 6)
                    nc.scalar.activation(val[s][:, t, :, 0:3:2, :], work[1 if t == 0 else 0][0:TP, :].rearrange(
                        "p (h o d) -> p h o d", o=2, d=HD), ACT.Copy).then_inc(v_copied, 1)

                def exp(b, g, t):
                    i = TT * g + t
                    act.wait_ge(scores_done, TT * NG * b + i + 1)
                    if t == 0:
                        need(act, pv_done, NG * b + g - 1)
                    nc.scalar.activation(prob[g % 2][:, t, :], score_ps[i % 2][0:TP, 0:GC], ACT.Exp,
                                         scale=SCORE_SCALE).then_inc(exp_done, 1)

                def sums(b, half):
                    act.wait_ge(pv_done, NG * b + 2 * half + 2)
                    need(act, divided, 4 * (2 * b + half - 1))
                    for odd in range(2):
                        for u in range(2):
                            q = HD * (2 * odd + u)
                            nc.scalar.activation(den[half][q:q + HD, :, :], by_pair(half, 32 + 32 * odd, u), ACT.Copy,
                                                 scale=1.0 + EPS_PROBS).then_inc(den_done, 1)

                def att_high(b):
                    act.wait_ge(att_sum, b + 1)
                    need(act, o_mm, b)
                    nc.scalar.activation(att_p[0][:], att_t[:], ACT.Copy).then_inc(att_hi, 1)

                def xn_high(b):
                    act.wait_ge(xn_tr, b + 1)
                    need(act, rows_stored, 32 * b)
                    nc.scalar.activation(xn_p[:, 0, :, :], work[1][:, 0:KT * S].rearrange("p (k s) -> p k s", k=KT),
                                         ACT.Copy).then_inc(xn_hi, 1)

                def x1_copy(b):
                    act.wait_ge(x1_tr, b + 1)
                    nc.scalar.activation(x1_t[:], work[1][:, 0:KT * S].rearrange("p (k s) -> p k s", k=KT),
                                         ACT.Copy).then_inc(x1_copied, 1)

                def iteration(b, s, attend, project, tail, ctx=True):
                    n, ns = b + 1, 1 - s
                    ex = (lambda g, t: exp(b, g, t)) if attend else (lambda g, t: None)
                    kh = (lambda m: key_hi(n, ns, m)) if project else (lambda m: None)
                    va = (lambda t: value(n, ns, t)) if project else (lambda t: None)
                    pieces = [(1 + LB * b + k, k, j) for k in range(LB) for j in range(NPAIR)] if attend else []
                    steps = iter(pieces)

                    def look(count):
                        for _ in range(count if attend else 0):
                            n_, k, j = next(steps)
                            lookup_pair(act, n_, k, LP, j)
                            if j == NPAIR - 1 and k == 1:
                                pass
                    ex(0, 0); look(1); ex(0, 1); look(1); kh(0); ex(0, 2); look(1)
                    ex(1, 0); look(1); ex(1, 1); look(1); kh(1); ex(1, 2); look(1)
                    if ctx:
                        split_ctx(b + 2, s)
                    ex(2, 0); look(1); kh(2); ex(2, 1); look(1)
                    ex(2, 2); kh(3)
                    if attend:
                        sums(b, 0)
                    look(1)
                    ex(3, 0); look(1); va(0); ex(3, 1); look(1); ex(3, 2)
                    if attend:
                        lookup_hi(act, 1 + LB * b, 0, LP)
                    look(2); va(1)
                    if tail:
                        xn_high(b - 1)
                    look(1); va(2)
                    look(2)
                    if attend:
                        sums(b, 1)
                    if tail:
                        x1_copy(b - 1)
                    if attend:
                        att_high(b)
                        lookup_hi(act, 2 + LB * b, 1, LP)

                split_ctx(0, 0)
                iteration(-1, 1, False, True, False)
                iteration(0, 0, True, True, False)
                iteration(1, 1, True, True, True)
                iteration(2, 0, True, True, True)
                with act.Fori(3, B - 4, 2) as i:
                    iteration(i, 1, True, True, True)
                    iteration(i + 1, 0, True, True, True)
                iteration(B - 3, 1, True, True, True)
                iteration(B - 2, 0, True, True, True, ctx=False)
                iteration(B - 1, 1, True, False, True, ctx=False)
                iteration(B, 0, False, False, True, ctx=False)

            @block.vector
            def _(dve):
                for s in range(2):
                    for i in range(2):
                        nc.vector.memset(ctx_t[s][i][:, :, T:TE].bitcast(fp32), 0.0).then_inc(zeroed, 1)
                for s in range(2):
                    nc.vector.memset(val[s][:, :, :, 1, :], 1.0).then_inc(zeroed, 1)
                nc.vector.memset(q_blk[:].bitcast(fp32), 0.0).then_inc(zeroed, 1)

                def clip(b, g, t):
                    dve.wait_ge(exp_done, TT * (NG * b + g) + t + 1)
                    p_ = prob[g % 2][:, t, :]
                    nc.vector.tensor_scalar(p_, p_, CLIP_LO, prob_cap[:, t, bass.ds(b, 1)], ALU.max, ALU.min)\
                        .then_inc(clip_done, 1)

                def key_lo(n, s, m):
                    dve.wait_ge(k_hi, NG * n + m + 1)
                    nc.vector.scalar_tensor_tensor(k_t[s][1][:, m, :], work[1 if m == 2 else 0][:, 0:TE],
                                                   bk[:, m:m + 1], k_t[s][0][:, m, :], ALU.add, ALU.subtract)\
                        .then_inc(k_lo, 1)

                def divide(b, half):
                    dve.wait_ge(den_done, 4 * (2 * b + half + 1))
                    nc.vector.reciprocal(den[half][:], den[half][:]).then_inc(inverted, 1)
                    dve.wait_ge(inverted, 2 * b + half + 1)
                    need(dve, att_lo, b)
                    for odd in range(2):
                        for u in range(2):
                            q = HD * (2 * odd + u)
                            nc.vector.tensor_tensor(att_t[q:q + HD, 2 * half:2 * half + 2, :],
                                                    by_pair(half, 96 * odd, u), den[half][q:q + HD, :, :],
                                                    ALU.mult).then_inc(divided, 1)

                def add_bv(b):
                    dve.wait_ge(divided, 8 * (b + 1))
                    nc.vector.tensor_tensor(att_t[:], att_t[:], bv[:].unsqueeze(2).broadcast_to([P, NG, S]), ALU.add)\
                        .then_inc(att_sum, 1)

                def att_low(b):
                    dve.wait_ge(att_hi, b + 1)
                    nc.vector.tensor_tensor(att_p[1][:], att_t[:], att_p[0][:], ALU.subtract).then_inc(att_lo, 1)

                def ln(b, k):
                    done = LN * b
                    if k == 0:
                        dve.wait_ge(o_mm, b + 1)
                        nc.vector.tensor_tensor(delta[:], work[1][0:S, :], bo[0:S, :], ALU.add).then_inc(ln_dve, 1)
                    elif k == 1:
                        dve.wait_ge(ln_dve, done + 1)
                        nc.vector.bn_stats(stats_b[:, 0, :], delta[:]).then_inc(ln_dve, 1)
                    elif k == 2:
                        need_apart(dve, ln_dve, done + 2)
                        nc.vector.bn_aggr(mv[:, 0, :], stats_b[:, 0, :]).then_inc(ln_dve, 1)
                    elif k == 3:
                        dve.wait_ge(ln_pool, LNP * b + 3)
                        nc.vector.tensor_scalar(delta[:], delta[:], mv[:, 0, 0:1], rs_b[:, 2:3], ALU.subtract, ALU.mult)\
                            .then_inc(ln_dve, 1)
                    elif k == 4:
                        dve.wait_ge(ln_dve, done + 4)
                        nc.vector.tensor_tensor(delta[:], delta[:], gamma[0:S, :], ALU.mult).then_inc(ln_dve, 1)
                    elif k == 5:
                        dve.wait_ge(ln_dve, done + 5)
                        dve.wait_ge(xb_done, b + 1)
                        need(dve, x1_tr, b)
                        nc.vector.tensor_tensor(x1[:], delta[:], xb[:], ALU.add).then_inc(ln_dve, 1)
                    elif k == 6:
                        dve.wait_ge(ln_dve, done + 6)
                        nc.vector.bn_stats(stats_b[:, 1, :], x1[:]).then_inc(ln_dve, 1)
                    elif k == 7:
                        need_apart(dve, ln_dve, done + 7)
                        nc.vector.bn_aggr(mv[:, 1, :], stats_b[:, 1, :]).then_inc(ln_dve, 1)
                    else:
                        dve.wait_ge(ln_pool, LNP * b + 5)
                        need(dve, xn_tr, b)
                        nc.vector.tensor_scalar(xn[:], x1[:], mv[:, 1, 0:1], rs_b[:, 4:5], ALU.subtract, ALU.mult)\
                            .then_inc(ln_dve, 1)

                def xn_low(b):
                    dve.wait_ge(xn_hi, b + 1)
                    nc.vector.tensor_tensor(xn_p[:, 1, :, :], work[1][:, 0:KT * S].rearrange("p (k s) -> p k s", k=KT),
                                            xn_p[:, 0, :, :], ALU.subtract).then_inc(xn_lo, 1)

                def iteration(b, s, attend, project, tail):
                    n, ns = b + 1, 1 - s
                    cl = (lambda g, t: clip(b, g, t)) if attend else (lambda g, t: None)
                    kl = (lambda m: key_lo(n, ns, m)) if project else (lambda m: None)
                    lns = (lambda *k: [ln(b - 1, x) for x in k]) if tail else (lambda *k: None)
                    steps = iter([(1 + LB * b + k, k, j) for k in range(LB) for j in range(1, NPAIR)])

                    def look(count):
                        for _ in range(count if attend else 0):
                            n_, k, j = next(steps)
                            lookup_pick(dve, n_, k, LP, j)
                    cl(0, 0); look(1); cl(0, 1); kl(0); cl(0, 2); look(1); lns(0)
                    cl(1, 0); look(1); lns(1, 2); cl(1, 1); kl(1); look(1); cl(1, 2); lns(3)
                    cl(2, 0); look(1); kl(2); lns(4); cl(2, 1); look(1); lns(5); cl(2, 2); kl(3); look(1)
                    if attend:
                        lookup_bits(dve, 2 + LB * b, 1, LP)
                        divide(b, 0)
                    lns(6, 7)
                    cl(3, 0); look(1); cl(3, 1); look(1); lns(8); cl(3, 2); look(2)
                    if tail:
                        xn_low(b - 1)
                    look(3)
                    if attend:
                        divide(b, 1)
                        if project:
                            next_bits(b + 1)
                        add_bv(b)
                        att_low(b)

                def next_bits(b):
                    dve.wait_ge(idx_loaded, 16 * (b + 1))
                    lookup_bits(dve, 1 + LB * b, 0, LP)

                next_bits(0)
                iteration(-1, 1, False, True, False)
                iteration(0, 0, True, True, False)
                iteration(1, 1, True, True, True)
                iteration(2, 0, True, True, True)
                with dve.Fori(3, B - 2, 2) as i:
                    iteration(i, 1, True, True, True)
                    iteration(i + 1, 0, True, True, True)
                iteration(B - 1, 1, True, False, True)
                iteration(B, 0, False, False, True)

            @block.gpsimd
            def _(pool):
                def split_ctx(n, s):
                    pool.wait_ge(ctx_hi, n + 1)
                    nc.gpsimd.tensor_tensor(ctx_t[s][1][:, :, 0:T], ctx_in[:], ctx_t[s][0][:, :, 0:T], ALU.subtract)\
                        .then_inc(ctx_lo, 1)

                def add_beta(b, s):
                    pool.wait_ge(x_loaded[s], 16 * ((b + 2 - s) // 2) if isinstance(b, int) else 8 * (b + 2 - s))
                    need(pool, ln_dve, LN * (b - 1) + 6)
                    nc.gpsimd.tensor_tensor(xb[:], xr[s][:], beta[0:S, :], ALU.add).then_inc(xb_done, 1)

                def rstd(b, which):
                    done = LNP * b
                    if which == 0:
                        need_apart(pool, ln_dve, LN * b + 3)
                        nc.gpsimd.tensor_scalar(rs_b[:, 0:1], mv[:, 0, 1:2], res[0:S, 1:2], EPS_LN, ALU.mult, ALU.add)\
                            .then_inc(ln_pool, 1)
                        pool.wait_ge(ln_pool, done + 1)
                        nc.gpsimd.tensor_tensor(rs_b[:, 1:2], rs_b[:, 0:1], neg_half[0:S, 0:1], ALU.pow)\
                            .then_inc(ln_pool, 1)
                        pool.wait_ge(ln_pool, done + 2)
                        nc.gpsimd.tensor_tensor(rs_b[:, 2:3], rs_b[:, 1:2], res[0:S, 0:1], ALU.mult).then_inc(ln_pool, 1)
                    else:
                        need_apart(pool, ln_dve, LN * b + 8)
                        nc.gpsimd.tensor_scalar(rs_b[:, 3:4], mv[:, 1, 1:2], EPS_LN, 1.0, ALU.add, ALU.mult)\
                            .then_inc(ln_pool, 1)
                        pool.wait_ge(ln_pool, done + 4)
                        nc.gpsimd.tensor_tensor(rs_b[:, 4:5], rs_b[:, 3:4], neg_half[0:S, 0:1], ALU.pow)\
                            .then_inc(ln_pool, 1)

                def iteration(b, s, attend, project, tail, ctx=True):
                    if tail:
                        add_beta(b - 1, 1 - s)
                        rstd(b - 1, 0)
                    if ctx:
                        split_ctx(b + 2, s)
                    if tail:
                        rstd(b - 1, 1)
                    if attend:
                        lookup_lo(pool, 1 + LB * b, 0, LP)
                        lookup_lo(pool, 2 + LB * b, 1, LP)

                split_ctx(0, 0)
                iteration(-1, 1, False, True, False)
                iteration(0, 0, True, True, False)
                iteration(1, 1, True, True, True)
                iteration(2, 0, True, True, True)
                with pool.Fori(3, B - 4, 2) as i:
                    iteration(i, 1, True, True, True)
                    iteration(i + 1, 0, True, True, True)
                iteration(B - 3, 1, True, True, True)
                iteration(B - 2, 0, True, True, True, ctx=False)
                iteration(B - 1, 1, True, False, True, ctx=False)
                iteration(B, 0, False, False, True, ctx=False)

            @block.sync
            def _(sp):
                def load_ctx(n):
                    need(sp, ctx_lo, n)
                    sp.dma_start(ctx_in[:], ins["ctx"][n]).then_inc(ctx_loaded, 16)

                def load_q(b):
                    need(sp, scores_done, TT * NG * b)
                    for j in range(HG):
                        sp.dma_start(q_blk[j * HD:(j + 1) * HD, :, :, j * S:(j + 1) * S].bitcast(fp32),
                                     q_dram[j * HD:(j + 1) * HD, :, :, bass.ds(b * S, S)]).then_inc(q_loaded, 16)

                def load_x(b, s):
                    need(sp, xb_done, b - 1)
                    sp.dma_start(xr[s][:], ins["x"][bass.ds(b * S, S), :]).then_inc(x_loaded[s], 16)

                def load_idx(b):
                    need(sp, bits_done, 3 * (1 + LB * b))
                    sp.dma_start(idx[:], ins["idx"][:, bass.ds(b * (LB * LP), LB * LP)]).then_inc(idx_loaded, 16)

                def store_rows(b):
                    sp.wait_ge(xn_lo, b + 1)
                    sp.dma_start(xn_dram[:, :, :, bass.ds(b * S, S)].rearrange("p a k s -> p (a k) s"),
                                 xn_p[:].rearrange("p a k s -> p (a k) s").bitcast(fp32)).then_inc(rows_stored, 16)
                    sp.wait_ge(x1_copied, b + 1)
                    sp.dma_start(x1_dram[:, :, bass.ds(b * S, S)], x1_t[:]).then_inc(rows_stored, 16)

                def iteration(b, s, attend, project, tail, ctx=True):
                    if ctx:
                        load_ctx(b + 3)
                    if project and attend:
                        load_idx(b + 1)
                    if attend:
                        lookup_store(sp, 1 + LB * b, LP, b * (LB * LP))
                    if project and attend:
                        load_q(b + 1)
                        load_x(b + 1, 1 - s)
                    if tail:
                        store_rows(b - 1)
                    if attend:
                        lookup_store(sp, 2 + LB * b, LP, b * (LB * LP) + LP)

                load_ctx(0)
                sp.wait_ge(zeroed, 7)
                load_q(0)
                load_idx(0)
                load_x(0, 0)
                load_ctx(1)
                iteration(-1, 1, False, True, False)
                iteration(0, 0, True, True, False)
                iteration(1, 1, True, True, True)
                iteration(2, 0, True, True, True)
                with sp.Fori(3, B - 4, 2) as i:
                    iteration(i, 1, True, True, True)
                    iteration(i + 1, 0, True, True, True)
                iteration(B - 3, 1, True, True, True, ctx=False)
                iteration(B - 2, 0, True, True, True, ctx=False)
                iteration(B - 1, 1, True, False, True, ctx=False)
                iteration(B, 0, False, False, True, ctx=False)
                sp.wait_ge(w_stored, 32 * (1 + LB * B))
                sp.wait_ge(rows_stored, 32 * B)
        att.close()

        ffn = ExitStack()
        wf = [sb(ffn, f"wf{i}", [P, WCOLS], fp32r) for i in range(2)]
        xf = [sb(ffn, f"xf{s}", [P, 2, KT, CH], fp32r) for s in range(2)]
        x1f = [sb(ffn, f"x1f{s}", [P, KT, CH]) for s in range(2)]
        silu = [sb(ffn, f"silu{s}", [P, CH]) for s in range(2)]
        hid = [sb(ffn, f"hid{s}", [P, CH]) for s in range(2)]
        hid_p = [[sb(ffn, f"hid_p{s}{i}", [P, CH], fp32r) for i in range(2)] for s in range(2)]

        wf_loaded = [sem(f"wf_loaded{j}") for j in range(JT)]
        xf_loaded = [sem(f"xf_loaded{s}") for s in range(2)]
        gate_mm = sem("gate_mm")
        up_mm = sem("up_mm")
        silu_done = sem("silu_done")
        hid_done = sem("hid_done")
        hid_hi = sem("hid_hi")
        hid_lo = sem("hid_lo")
        down_mm = sem("down_mm")
        down_all = sem("down_all")
        y_done = sem("y_done")
        y_stored = [sem(f"y_stored{s}") for s in range(2)]
        gate_ps, up_ps = work, score_ps
        acc = pv_ps + pair_ps
        PARTS = ((0, 0), (0, 1), (1, 0))
        FREE = 2

        def gate_w(a, j, k):
            return wf[a][:, JCOL[j] + k * JW[j]:JCOL[j] + (k + 1) * JW[j]]

        def up_w(a, j, k):
            return wf[a][:, JCOL[j] + (KT + k) * JW[j]:JCOL[j] + (KT + k + 1) * JW[j]]

        def down_w(a, j, m):
            at = JCOL[j] + 2 * KT * JW[j] + m * P
            return wf[a][0:JW[j], at:at + P]

        with nc.Block() as block:
            @block.sync
            def _(sp):
                def load_rows(c, s):
                    sp.dma_start(xf[s][:].rearrange("p a k s -> p (a k) s").bitcast(fp32),
                                 xn_dram[:, :, :, bass.ds(c * CH, CH)].rearrange("p a k s -> p (a k) s"))\
                        .then_inc(xf_loaded[s], 16)
                    sp.dma_start(x1f[s][:], x1_dram[:, :, bass.ds(c * CH, CH)]).then_inc(xf_loaded[s], 16)
                load_rows(0, 0)
                for j in range(JT):
                    end = JCOL[j + 1] if j + 1 < JT else WCOLS
                    for a in range(2):
                        sp.dma_start(wf[a][:, JCOL[j]:end].bitcast(fp32), w_dram[:, a, JCOL[j]:end]).then_inc(wf_loaded[j], 16)
                    if j == 1:
                        load_rows(1, 1)
                for c in range(NC):
                    s = c % 2
                    sp.wait_ge(y_done, KT * (c + 2))
                    sp.dma_start(out_t[:, :, c * CH:(c + 1) * CH].rearrange("k p s -> p k s"), x1f[s][:])\
                        .then_inc(y_stored[s], 16)
                    if c + 2 < NC:
                        sp.wait_ge(y_stored[s], 16 * (c // 2 + 1))
                        load_rows(c + 2, s)
                for s in range(2):
                    sp.wait_ge(y_stored[s], 16 * NC // 2)

            @block.tensor
            def _(pe):
                def up_units(c, s, j):
                    w = JW[j]
                    if j == 0:
                        pe.wait_ge(xf_loaded[s], 16 * (c + 2 - s))
                    pe.wait_ge(wf_loaded[j], 32)
                    for name, bank, wts, n_of, free, at in (
                            ("gate", gate_ps, gate_w, gate_mm, silu_done, JT * c + j - (j > 0) + FREE),
                            ("up", up_ps, up_w, up_mm, hid_done, JT * c + j - (j > 0) + FREE)):
                        pe.wait_ge(free, at)
                        for n, (a, b) in enumerate(PARTS):
                            for k in range(KT):
                                mm = nc.tensor.matmul(bank[j % 2][0:w, 0:CH], wts(a, j, k), xf[s][:, b, k, :],
                                                      start=(n == 0 and k == 0), stop=(n == 2 and k == KT - 1))
                        mm.then_inc(n_of, 1)

                def down_units(c, s, j):
                    w = JW[j]
                    pe.wait_ge(hid_lo, JT * c + j + 1 + FREE)
                    if j == 0:
                        pe.wait_ge(y_done, KT * (c + 1))
                    for m in range(KT):
                        for n, (a, b) in enumerate(PARTS):
                            mm = nc.tensor.matmul(acc[m][:, 0:CH], down_w(a, j, m), hid_p[j % 2][b][0:w, :],
                                                  start=(j == 0 and n == 0), stop=(j == JT - 1 and n == 2))
                    mm.then_inc(down_mm, 1)

                def chunk(c, s):
                    for j in range(JT):
                        up_units(c, s, j)
                        if j > 0:
                            down_units(c, s, j - 1)
                    down_units(c, s, JT - 1)

                pe.sem_inc(down_mm, FREE)
                with pe.Fori(0, NC - 1, 2) as c:
                    chunk(c, 0)
                    chunk(c + 1, 1)

            @block.scalar
            def _(act):
                def silu_of(c, j):
                    w = JW[j]
                    act.wait_ge(gate_mm, JT * c + j + 1)
                    act.wait_ge(hid_done, JT * c + j - (j > 0) + FREE)
                    nc.scalar.activation(silu[j % 2][0:w, :], gate_ps[j % 2][0:w, 0:CH], ACT.Silu).then_inc(silu_done, 1)

                def high_of(c, j):
                    w = JW[j]
                    act.wait_ge(hid_done, JT * c + j + 1 + FREE)
                    act.wait_ge(down_mm, JT * c + j - (j > 0) + FREE)
                    nc.scalar.activation(hid_p[j % 2][0][0:w, :], hid[j % 2][0:w, :], ACT.Copy).then_inc(hid_hi, 1)

                act.sem_inc(silu_done, FREE)
                with act.Fori(0, NC, 1) as c:
                    for j in range(JT):
                        silu_of(c, j)
                        high_of(c, j)

            @block.vector
            def _(dve):
                def chunk(c, s):
                    for j in range(JT):
                        w = JW[j]
                        dve.wait_ge(silu_done, JT * c + j + 1 + FREE)
                        dve.wait_ge(up_mm, JT * c + j + 1)
                        dve.wait_ge(hid_lo, JT * c + j - (j > 0) + FREE)
                        nc.vector.tensor_tensor(hid[j % 2][0:w, :], silu[j % 2][0:w, :], up_ps[j % 2][0:w, 0:CH],
                                                ALU.mult).then_inc(hid_done, 1)
                        dve.wait_ge(hid_hi, JT * c + j + 1)
                        nc.vector.tensor_tensor(hid_p[j % 2][1][0:w, :], hid[j % 2][0:w, :], hid_p[j % 2][0][0:w, :],
                                                ALU.subtract).then_inc(hid_lo, 1)
                    dve.wait_ge(down_mm, JT * (c + 1) + FREE)
                    for m in range(KT):
                        nc.vector.scalar_tensor_tensor(x1f[s][:, m, :], acc[m][:, 0:CH], tanh_g[:, 1:2], x1f[s][:, m, :],
                                                       ALU.mult, ALU.add).then_inc(y_done, 1)
                dve.sem_inc(hid_done, FREE)
                dve.sem_inc(hid_lo, FREE)
                dve.sem_inc(y_done, KT)
                with dve.Fori(0, NC - 1, 2) as c:
                    chunk(c, 0)
                    chunk(c + 1, 1)
        ffn.close()


def kernel(**inputs):
    import numpy as np
    import concourse.bacc as bacc
    from concourse import mybir as mb
    from concourse.bass_utils import run_bass_kernel_spmd

    a = {k: np.asarray(v) for k, v in inputs.items()}
    quad = [0, 2, 1, 3]
    order = np.concatenate([np.arange(HD) + HD * (HG * g + quad[q]) for g in range(NG) for q in range(HG)])

    def rows(v):
        return np.ascontiguousarray(np.broadcast_to(v.reshape(1, -1), (P, v.size)))

    def feature_major(w):
        return np.ascontiguousarray(w.T.reshape(KT, P, -1).transpose(1, 0, 2))

    def columns(v):
        return np.ascontiguousarray(v.reshape(KT, P).T)

    gate, up, down = (a["L0_ffn_" + n] for n in ("gate_idx", "up_idx", "down_idx"))
    gate_f, up_f = feature_major(gate), feature_major(up)
    blocks = []
    for j in range(JT):
        cols = slice(j * P, j * P + JW[j])
        blocks += [gate_f[:, :, cols].reshape(P, -1), up_f[:, :, cols].reshape(P, -1)]
        tile = np.zeros((P, H), down.dtype)
        tile[:JW[j]] = down.T[cols]
        blocks.append(tile)
    arrays = {
        "x": np.ascontiguousarray(a["x"].reshape(ROWS, H)),
        "x4": np.ascontiguousarray(a["x"].reshape(NC, CB, S, H).transpose(0, 2, 1, 3)),
        "ctx": np.ascontiguousarray(a["ctx_2048"].reshape(B, T, KT, P).transpose(0, 3, 2, 1)),
        "mask": np.ascontiguousarray(a["mask_BxS2_ik0"].reshape(B, TT, TP).transpose(2, 1, 0)),
        "wq": feature_major(a["L0_xattn_Wq"]),
        "wk": feature_major(a["L0_xattn_Wk"]),
        "wv": feature_major(a["L0_xattn_Wv"]),
        "wo": feature_major(a["L0_xattn_Wo"][:, order]),
        "bq": columns(a["L0_xattn_bq"]),
        "bk": columns(a["L0_xattn_bk"]),
        "bv": columns(a["L0_xattn_bv"][order]),
        "bo": rows(a["L0_xattn_bo"]),
        "gamma": rows(a["L0_xattn_ln_gamma"]),
        "beta": rows(a["L0_xattn_ln_beta"]),
        "lut": rows(a["L0_ffn_lut"]),
        "g_xattn": rows(a["g_xattn"]),
        "g_ffn": rows(a["g_ffn"]),
        "res": rows(a["L0_xattn_residual_scale"].reshape(1)),
        "idx": np.ascontiguousarray(np.concatenate(blocks, axis=1)),
    }
    nc = bacc.Bacc("TRN2", target_bir_lowering=False, num_devices=1)
    ins = {n: nc.dram_tensor(f"in_{n}", v.shape, mb.dt.from_np(v.dtype), kind="ExternalInput").ap()
           for n, v in arrays.items()}
    out_t = nc.dram_tensor("out_t", (KT, P, ROWS), mb.dt.float32, kind="ExternalOutput").ap()
    flamingo_kernel(nc, ins, out_t)
    r = run_bass_kernel_spmd(nc, [{f"in_{n}": v for n, v in arrays.items()}], core_ids=[0])
    got = r.results[0]["out_t"]
    return np.ascontiguousarray(got.reshape(H, ROWS).T).reshape(B, S, H)
```

```python
from contextlib import ExitStack

import concourse.bass as bass
from concourse import mybir

B, S, T, H, NH = 16, 112, 375, 512, 16
INTER = 1376
P = 128
HD = H // NH
KT = H // P
HG = P // HD
NG = NH // HG
TT = 3
TP = T // TT
TE = T + 1
ROWS = B * S
CB = 4
NC = B // CB
CH = CB * S
GC = HG * S
JT = -(-INTER // P)
JW = [min(P, INTER - j * P) for j in range(JT)]
JCOL = [j * (2 * KT * P + H) for j in range(JT)]
WCOLS = JCOL[-1] + 2 * KT * JW[-1] + H
LP = 448
LB = 2
LW = LB * LP
LREST = WCOLS - B * LW
PRE = [min(LW, LREST - i * LW) for i in range(-(-LREST // LW))]
LPRE = sum(-(-w // LP) for w in PRE)
PER_M = -(-LPRE * 8 // (NC * KT))
LUT = 16
NPAIR = LUT // 2
MASK_BITS = 14
EPS_LN = 1e-5
EPS_PROBS = 1e-8
SCORE_SCALE = HD ** -0.5
CLIP_HI = float(2.718281828459045 ** 50.0)
CLIP_LO = float(2.718281828459045 ** -50.0)
RES_MAX = 0.3


def flamingo_kernel(nc, ins, out_t):
    fp32, fp32r, bf16 = mybir.dt.float32, mybir.dt.float32r, mybir.dt.bfloat16
    i32, u16 = mybir.dt.int32, mybir.dt.uint16
    ALU = mybir.AluOpType
    ACT = mybir.ActivationFunctionType

    def need(engine, sem, value):
        if isinstance(value, int) and value <= 0:
            return
        assert isinstance(value, int) or value.min_val > 0
        engine.wait_ge(sem, value)

    def need_apart(engine, sem, value):
        need(engine, sem, value)
        engine.nop(nofuse=True)

    q_dram = nc.dram_tensor("q_parts", (P, 2, NG, ROWS), fp32, kind="Internal").ap()
    w_dram = nc.dram_tensor("w_parts", (P, 2, WCOLS), fp32, kind="Internal").ap()
    xn_dram = nc.dram_tensor("xn_parts", (P, 2, KT, ROWS), fp32, kind="Internal").ap()
    x1_dram = nc.dram_tensor("x1_rows_t", (P, KT, ROWS), fp32, kind="Internal").ap()

    top = ExitStack()
    with top:
        def sb(stack, name, shape, dt=fp32):
            return stack.enter_context(nc.sbuf_tensor(name, shape, dt))

        def ps(stack, name, shape, dt=fp32):
            return stack.enter_context(nc.psum_tensor(name, shape, dt))

        def sem(name):
            return top.enter_context(nc.semaphore(name))

        work = [ps(top, f"work{i}", [P, 512]) for i in range(2)]
        score_ps = [ps(top, f"score_ps{i}", [P, 512]) for i in range(2)]
        pv_ps = [ps(top, f"pv_ps{i}", [P, 512]) for i in range(2)]
        pair_ps = [ps(top, f"pair_ps{i}", [P, 512]) for i in range(2)]

        ident = sb(top, "ident", [P, P])
        neg_half = sb(top, "neg_half", [P, CB])
        lut = sb(top, "lut", [P, LUT])
        lut_step = sb(top, "lut_step", [P, NPAIR])
        gates = sb(top, "gates", [P, 2])
        tanh_g = sb(top, "tanh_g", [P, 2])
        res = sb(top, "res", [P, 2])

        att = ExitStack()
        wk = [sb(att, f"wk{i}", [P, KT, H], fp32r) for i in range(2)]
        wv = [sb(att, f"wv{i}", [P, KT, H], fp32r) for i in range(2)]
        wo = [sb(att, f"wo{i}", [P, KT, H], fp32r) for i in range(2)]
        bq = sb(att, "bq", [P, KT])
        bk = sb(att, "bk", [P, KT])
        bv = sb(att, "bv", [P, NG])
        bo = sb(att, "bo", [P, H])
        gamma = sb(att, "gamma", [P, H])
        beta = sb(att, "beta", [P, H])
        mask = sb(att, "mask", [TP, TT, B], i32)
        prob_cap = sb(att, "prob_cap", [TP, TT, B])
        idx = sb(att, "idx", [P, LW], i32)
        bit0 = sb(att, "bit0", [P, LW], u16)
        pair_id = sb(att, "pair_id", [P, LW], u16)
        pair_mask = sb(att, "pair_mask", [P, NPAIR, LW], u16)
        w_val = [sb(att, f"w_val{i}", [P, LP]) for i in range(2)]
        w_hi = [sb(att, f"w_hi{i}", [P, LP], fp32r) for i in range(2)]
        w_lo = [sb(att, f"w_lo{i}", [P, LP], fp32r) for i in range(2)]

        pre = ExitStack()
        stage = [sb(pre, f"stage{i}", [P, KT, H]) for i in range(2)]
        wq = [sb(pre, f"wq{i}", [P, KT, H], fp32r) for i in range(2)]
        xq = [sb(pre, f"xq{i}", [S, CB, H]) for i in range(2)]
        qstats = sb(pre, "qstats", [S, CB, 6])
        qmv = sb(pre, "qmv", [S, CB, 2])
        qvar = sb(pre, "qvar", [S, CB])
        qrstd = sb(pre, "qrstd", [S, CB])
        hs = sb(pre, "hs", [S, CB, H])
        hs_t = [[sb(pre, f"hs_t{s}{i}", [P, KT, CH], fp32r) for i in range(2)] for s in range(2)]
        qneg = sb(pre, "qneg", [S, CB])
        bv_p = [sb(pre, f"bv_p{i}", [P, KT, S], fp32r) for i in range(2)]
        q_out = sb(pre, "q_out", [P, 2, 2, CH], fp32r)

        c_const = sem("c_const")
        c_mask = sem("c_mask")
        c_w = [sem(f"c_w{i}") for i in range(2)]
        c_x = [sem(f"c_x{i}") for i in range(2)]
        c_idx = sem("c_idx")
        c_ident = sem("c_ident")
        neg_half_set = sem("neg_half_set")
        tanh_done = sem("tanh_done")
        consts_done = sem("consts_done")
        cap_done = sem("cap_done")
        wsplit_hi = sem("wsplit_hi")
        wq_lo = sem("wq_lo")
        w_lo_pool = sem("w_lo_pool")
        bv_split = sem("bv_split")
        bo_mm = sem("bo_mm")
        q_stats = sem("q_stats")
        q_rstd = sem("q_rstd")
        q_pool = sem("q_pool")
        hs_done = sem("hs_done")
        hs_tr = sem("hs_tr")
        hs_hi = sem("hs_hi")
        hs_lo = sem("hs_lo")
        q_mm = sem("q_mm")
        q_hi = sem("q_hi")
        q_lo = sem("q_lo")
        q_stored = [sem(f"q_stored{i}") for i in range(2)]
        bits_done = sem("bits_done")
        masks_done = sem("masks_done")
        pair_done = sem("pair_done")
        base_done = sem("base_done")
        picked = sem("picked")
        w_hi_done = sem("w_hi_done")
        w_lo_done = sem("w_lo_done")
        w_stored = [sem(f"w_stored{i}") for i in range(2)]

        def lookup_masks(dve, r, n, width):
            need(dve, pair_done, NPAIR * n)
            low = idx[:].bitcast(u16)[:, 0:2 * width:2]
            nc.vector.tensor_scalar(bit0[:, 0:width], low, 1, None, ALU.bitwise_and).then_inc(bits_done, 1)
            nc.vector.tensor_scalar(pair_id[:, 0:width], low, MASK_BITS, None, ALU.bitwise_and).then_inc(bits_done, 1)
            need(dve, picked, 7 * n)
            dve.wait_ge(bits_done, 2 * r + 2)
            for j in range(1, NPAIR):
                nc.vector.tensor_scalar(pair_mask[:, j, 0:width], pair_id[:, 0:width], float(2 * j), None,
                                        ALU.is_equal).then_inc(masks_done, 1)

        def lookup_pair(act, r, n, k, width, j):
            part = slice(k * LP, k * LP + width)
            if j == 0:
                act.wait_ge(bits_done, 2 * r + 1)
                need(act, w_lo_done, n - 1)
                nc.scalar.activation(w_val[k][:, 0:width], bit0[:, part], ACT.Identity,
                                     scale=lut_step[:, 0:1], bias=lut[:, 0:1]).then_inc(pair_done, 1)
                return
            need(act, picked, 7 * n + j - 2)
            nc.scalar.activation(pair_ps[(k + j) % 2][:, 0:width], bit0[:, part], ACT.Identity,
                                 scale=lut_step[:, j:j + 1], bias=lut[:, 2 * j:2 * j + 1]).then_inc(pair_done, 1)

        def lookup_pick(dve, r, n, k, width, j):
            if j == 1 and k == 0:
                dve.wait_ge(masks_done, 7 * (r + 1))
            if j > 1:
                dve.wait_ge(picked, 7 * n + j - 1)
            need_apart(dve, pair_done, NPAIR * n + j + 1)
            nc.vector.copy_predicated(w_val[k][:, 0:width], pair_mask[:, j, k * LP:k * LP + width],
                                      pair_ps[(k + j) % 2][:, 0:width]).then_inc(picked, 1)

        def lookup_hi(act, r, n, k, width):
            act.wait_ge(picked, 7 * (n + 1))
            need(act, w_stored[k], 32 * r)
            nc.scalar.activation(w_hi[k][:, 0:width], w_val[k][:, 0:width], ACT.Copy).then_inc(w_hi_done, 1)

        def lookup_lo(pool, n, k, width):
            pool.wait_ge(w_hi_done, n + 1)
            nc.gpsimd.tensor_tensor(w_lo[k][:, 0:width], w_val[k][:, 0:width], w_hi[k][:, 0:width],
                                    ALU.subtract).then_inc(w_lo_done, 1)

        def lookup_store(sp, n, k, width, col):
            sp.wait_ge(w_lo_done, n + 1)
            sp.dma_start(w_dram[:, 0, bass.ds(col, width)], w_hi[k][:, 0:width].bitcast(fp32))\
                .then_inc(w_stored[k], 16)
            sp.dma_start(w_dram[:, 1, bass.ds(col, width)], w_lo[k][:, 0:width].bitcast(fp32))\
                .then_inc(w_stored[k], 16)

        pre_pieces, col = [], B * LW
        for r, total in enumerate(PRE):
            for k in range(-(-total // LP)):
                pre_pieces.append((r, len(pre_pieces), k, min(LP, total - k * LP), col))
                col += pre_pieces[-1][3]
        assert len(pre_pieces) == LPRE and all(-(-w // LP) == LB for w in PRE)

        N_CONST = 11
        pre_steps = [(r, n, k, w, j) for r, n, k, w, _ in pre_pieces for j in range(NPAIR)]
        hs_banks = score_ps + pv_ps
        with nc.Block() as block:
            @block.sync
            def _(sp):
                sp.dma_start(xq[0][:], ins["x4"][0]).then_inc(c_x[0], 16)
                sp.dma_start(stage[0][:], ins["wq"]).then_inc(c_w[0], 16)
                sp.dma_start(idx[:, 0:PRE[0]], ins["idx"][:, B * LW:B * LW + PRE[0]]).then_inc(c_idx, 16)
                sp.dma_start(xq[1][:], ins["x4"][1]).then_inc(c_x[1], 16)
                for tile, name in ((bq, "bq"), (bk, "bk"), (bv, "bv"), (bo, "bo"), (gamma, "gamma"), (beta, "beta"),
                                   (lut, "lut")):
                    sp.dma_start(tile[:], ins[name]).then_inc(c_const, 16)
                sp.dma_start(gates[:, 0:1], ins["g_xattn"]).then_inc(c_const, 16)
                sp.dma_start(gates[:, 1:2], ins["g_ffn"]).then_inc(c_const, 16)
                sp.dma_start(res[:, 0:1], ins["res"]).then_inc(c_const, 16)
                sp.dma_start(mask[:], ins["mask"]).then_inc(c_const, 16)
                sp.dma_start(stage[1][:], ins["wk"]).then_inc(c_w[1], 16)
                sp.wait_ge(wq_lo, 1)
                sp.dma_start(stage[0][:], ins["wv"]).then_inc(c_w[0], 16)
                sp.wait_ge(hs_done, CB)
                sp.dma_start(xq[0][:], ins["x4"][2]).then_inc(c_x[0], 16)
                stores = iter(pre_pieces)
                stored = [0]

                def store_next():
                    lookup_store(sp, *next(stores)[1:])
                for c in range(NC):
                    for m in range(KT):
                        sp.wait_ge(q_lo, KT * c + m + 1)
                        sp.dma_start(q_dram[:, :, m, bass.ds(c * CH, CH)], q_out[:, m % 2, :, :].bitcast(fp32))\
                            .then_inc(q_stored[m % 2], 16)
                        if m == 2 and c == 0:
                            sp.wait_ge(w_lo_pool, 1)
                            sp.dma_start(stage[1][:], ins["wo"]).then_inc(c_w[1], 16)
                        if m == 3 and c == 0:
                            sp.wait_ge(hs_done, 2 * CB)
                            sp.dma_start(xq[1][:], ins["x4"][3]).then_inc(c_x[1], 16)
                        if m == 3 and c < len(PRE) - 1:
                            sp.wait_ge(bits_done, 2 * (c + 1))
                            sp.dma_start(idx[:, 0:PRE[c + 1]], ins["idx"][:, (B + c + 1) * LW:(B + c + 1) * LW + PRE[c + 1]])\
                                .then_inc(c_idx, 16)
                        done = ((KT * c + m) * PER_M - NPAIR + 1) // NPAIR
                        while done > stored[0] and stored[0] < LPRE:
                            store_next()
                            stored[0] += 1
                while stored[0] < LPRE:
                    store_next()
                    stored[0] += 1
                for i in range(2):
                    sp.wait_ge(q_stored[i], 16 * NC * KT // 2)

            @block.gpsimd
            def _(pool):
                nc.gpsimd.memset(ident[:], 0.0).then_inc(c_ident, 1)
                nc.gpsimd.memset(neg_half[:], -0.5).then_inc(neg_half_set, 1)
                pool.wait_ge(c_ident, 1)
                nc.gpsimd.affine_select(out=ident[:], in_=ident[:], compare_op=ALU.not_equal, fill=1.0, base=0,
                                        pattern=[[-1, P]], channel_multiplier=1).then_inc(c_ident, 1)
                pool.wait_ge(neg_half_set, 1)

                def normalise(c):
                    pool.wait_ge(q_stats, 2 * CB * (c + 1))
                    nc.gpsimd.tensor_scalar(qvar[:], qmv[:, :, 1], EPS_LN, 1.0, ALU.add, ALU.mult).then_inc(q_pool, 1)
                    nc.gpsimd.tensor_scalar(qneg[:], qmv[:, :, 0], -1.0, 0.0, ALU.mult, ALU.add).then_inc(q_pool, 1)
                    pool.wait_ge(q_pool, 2 * (c + 1))
                    nc.gpsimd.tensor_tensor(qrstd[:], qvar[:], neg_half[0:S, :], ALU.pow).then_inc(q_rstd, 1)
                    pool.wait_ge(q_rstd, c + 1)
                    need(pool, hs_tr, KT * c)
                    for i in range(CB):
                        nc.gpsimd.tensor_scalar(hs[:, i, :], xq[c % 2][:, i, :], qneg[:, i:i + 1], qrstd[:, i:i + 1],
                                                ALU.add, ALU.mult).then_inc(hs_done, 1)

                def split_lo(i, dst):
                    pool.wait_ge(wsplit_hi, i + 1)
                    nc.gpsimd.tensor_tensor(dst[1][:], stage[i % 2][:], dst[0][:], ALU.subtract).then_inc(w_lo_pool, 1)
                low = iter(pre_pieces)
                normalise(0)
                normalise(1)
                split_lo(1, wk)
                normalise(2)
                for _ in range(1):
                    _, n, k, width, _ = next(low)
                    lookup_lo(pool, n, k, width)
                split_lo(2, wv)
                _, n, k, width, _ = next(low)
                lookup_lo(pool, n, k, width)
                normalise(3)
                split_lo(3, wo)
                for _, n, k, width, _ in low:
                    lookup_lo(pool, n, k, width)

            @block.scalar
            def _(act):
                def split_hi(i, dst):
                    act.wait_ge(c_w[i % 2], 16 * (i // 2 + 1))
                    nc.scalar.activation(dst[0][:], stage[i % 2][:], ACT.Copy).then_inc(wsplit_hi, 1)

                def hs_high(c):
                    for k in range(KT):
                        act.wait_ge(hs_tr, KT * c + k + 1)
                        if k == 0:
                            need(act, q_mm, KT * (c - 1))
                        nc.scalar.activation(hs_t[c % 2][0][:, k, :], hs_banks[k][:, 0:CH], ACT.Copy).then_inc(hs_hi, 1)

                steps = iter(pre_steps)

                def look(count):
                    for _ in range(count):
                        step = next(steps, None)
                        if step:
                            lookup_pair(act, *step)
                            if step[4] == NPAIR - 2 and step[1] > 0:
                                lookup_hi(act, *pre_pieces[step[1] - 1][:4])
                split_hi(0, wq)
                act.wait_ge(c_const, 16 * N_CONST)
                nc.scalar.activation(tanh_g[:], gates[:], ACT.Tanh).then_inc(tanh_done, 1)
                nc.scalar.activation(bv_p[0][:], bv[:].unsqueeze(2).broadcast_to([P, KT, S]), ACT.Copy).then_inc(bv_split, 1)
                hs_high(0)
                split_hi(1, wk)
                act.wait_ge(consts_done, 1)
                for c in range(NC):
                    for m in range(KT):
                        if m == 2 and c + 1 < NC:
                            hs_high(c + 1)
                        act.wait_ge(q_mm, KT * c + m + 1)
                        need(act, q_stored[m % 2], 16 * ((KT * c + m) // 2))
                        nc.scalar.activation(q_out[:, m % 2, 0, :], work[m % 2][:, 0:CH], ACT.Identity,
                                             bias=bq[:, m:m + 1]).then_inc(q_hi, 1)
                        look(PER_M)
                    if c < 2:
                        split_hi(c + 2, (wv, wo)[c])
                look(len(pre_steps))
                lookup_hi(act, *pre_pieces[-1][:4])

            @block.vector
            def _(dve):
                def stats(c):
                    dve.wait_ge(c_x[c % 2], 16 * (c // 2 + 1))
                    for i in range(CB):
                        nc.vector.bn_stats(qstats[:, i, :], xq[c % 2][:, i, :]).then_inc(q_stats, 1)
                    dve.wait_ge(q_stats, 2 * CB * c + CB)
                    need(dve, hs_done, CB * c)
                    for i in range(CB):
                        nc.vector.bn_aggr(qmv[:, i, :], qstats[:, i, :]).then_inc(q_stats, 1)

                def hs_low(c):
                    for k in range(KT):
                        dve.wait_ge(hs_hi, KT * c + k + 1)
                        nc.vector.tensor_tensor(hs_t[c % 2][1][:, k, :], hs_banks[k][:, 0:CH], hs_t[c % 2][0][:, k, :],
                                                ALU.subtract).then_inc(hs_lo, 1)

                def masks(r):
                    dve.wait_ge(c_idx, 16 * (r + 1))
                    lookup_masks(dve, r, LB * r, PRE[r])
                steps = iter(pre_steps)

                def look(count):
                    for _ in range(count):
                        r, n, k, width, j = next(steps, (0, 0, 0, 0, 0))
                        if j > 0:
                            lookup_pick(dve, r, n, k, width, j)
                        if j == NPAIR - 1 and k == LB - 1 and r + 1 < len(PRE):
                            masks(r + 1)
                stats(0)
                dve.wait_ge(wsplit_hi, 1)
                nc.vector.tensor_tensor(wq[1][:], stage[0][:], wq[0][:], ALU.subtract).then_inc(wq_lo, 1)
                hs_low(0)
                stats(1)
                dve.wait_ge(c_const, 16 * N_CONST)
                nc.vector.tensor_tensor(lut_step[:], lut[:, 1:LUT:2], lut[:, 0:LUT:2], ALU.subtract).then_inc(consts_done, 1)
                masks(0)
                nc.vector.tensor_scalar(res[:, 0:1], res[:, 0:1], 0.0, RES_MAX, ALU.max, ALU.min).then_inc(cap_done, 1)
                dve.wait_ge(tanh_done, 1)
                nc.vector.tensor_scalar(gamma[:], gamma[:], tanh_g[:, 0:1], None, ALU.mult).then_inc(cap_done, 1)
                nc.vector.tensor_scalar(beta[:], beta[:], tanh_g[:, 0:1], None, ALU.mult).then_inc(cap_done, 1)
                dve.wait_ge(cap_done, 1)
                nc.vector.tensor_tensor(res[:, 1:2], res[:, 0:1], res[:, 0:1], ALU.mult).then_inc(cap_done, 1)
                nc.vector.tensor_scalar(prob_cap[:], mask[:], 0.5, CLIP_HI, ALU.is_gt, ALU.mult).then_inc(cap_done, 1)
                dve.wait_ge(cap_done, 5)
                nc.vector.tensor_scalar(prob_cap[:], prob_cap[:], CLIP_LO, None, ALU.max).then_inc(cap_done, 1)
                dve.wait_ge(bv_split, 1)
                nc.vector.tensor_tensor(bv_p[1][:], bv[:].unsqueeze(2).broadcast_to([P, KT, S]), bv_p[0][:], ALU.subtract)\
                    .then_inc(bv_split, 1)
                for c in range(NC):
                    for m in range(KT):
                        if m == 2 and c + 1 < NC:
                            hs_low(c + 1)
                        dve.wait_ge(q_hi, KT * c + m + 1)
                        nc.vector.scalar_tensor_tensor(q_out[:, m % 2, 1, :], work[m % 2][:, 0:CH], bq[:, m:m + 1],
                                                       q_out[:, m % 2, 0, :], ALU.add, ALU.subtract).then_inc(q_lo, 1)
                        look(PER_M)
                        if m == 2 and c + 2 < NC:
                            stats(c + 2)
                look(len(pre_steps))
                dve.wait_ge(bo_mm, 1)
                nc.vector.tensor_tensor(bo[0:S, :], work[0][0:S, :], bo[0:S, :], ALU.add).then_inc(cap_done, 1)

            @block.tensor
            def _(pe):
                def transposes(c):
                    pe.wait_ge(hs_done, CB * (c + 1))
                    need(pe, hs_lo, KT * c)
                    for k in range(KT):
                        for i in range(CB):
                            mm = nc.tensor.transpose(hs_banks[k][:, i * S:(i + 1) * S], hs[:, i, k * P:(k + 1) * P],
                                                     ident[0:S, 0:S])
                        mm.then_inc(hs_tr, 1)
                pe.wait_ge(c_ident, 2)
                transposes(0)
                pe.wait_ge(wq_lo, 1)
                for c in range(NC):
                    pe.wait_ge(hs_lo, KT * (c + 1))
                    for m in range(KT):
                        if m == 2 and c + 1 < NC:
                            transposes(c + 1)
                        need(pe, q_lo, KT * c + m - 1)
                        for n, (a, b) in enumerate(((0, 0), (0, 1), (1, 0))):
                            for k in range(KT):
                                mm = nc.tensor.matmul(work[m % 2][:, 0:CH], wq[a][:, k, m * P:(m + 1) * P],
                                                      hs_t[c % 2][b][:, k, :], start=(n == 0 and k == 0),
                                                      stop=(n == 2 and k == KT - 1))
                        mm.then_inc(q_mm, 1)
                pe.wait_ge(w_lo_pool, 3)
                pe.wait_ge(bv_split, 2)
                pe.wait_ge(q_lo, KT * NC - 1)
                for n, (a, b) in enumerate(((0, 0), (0, 1), (1, 0))):
                    for k in range(KT):
                        mm = nc.tensor.matmul(work[0][0:S, :], bv_p[a][:, k, :], wo[b][:, k, :],
                                              start=(n == 0 and k == 0), stop=(n == 2 and k == KT - 1))
                mm.then_inc(bo_mm, 1)
        pre.close()

        ctx_in = sb(att, "ctx_in", [P, KT, T])
        ctx_t = [[sb(att, f"ctx_t{s}{i}", [P, KT, TE], fp32r) for i in range(2)] for s in range(2)]
        k_t = [[sb(att, f"k_t{s}{i}", [P, NG, TE], fp32r) for i in range(2)] for s in range(2)]
        val = [sb(att, f"val{s}", [TP, TT, NH // 2, 3, HD]) for s in range(2)]
        q_blk = sb(att, "q_blk", [P, 2, NG, GC], fp32r)
        prob = [sb(att, f"prob{s}", [TP, TT, GC]) for s in range(2)]
        den = [sb(att, f"den{s}", [P, 2, S]) for s in range(2)]
        att_t = sb(att, "att_t", [P, NG, S])
        att_p = [sb(att, f"att_p{i}", [P, NG, S], fp32r) for i in range(2)]
        xr = [sb(att, f"xr{s}", [S, H]) for s in range(2)]
        xb = sb(att, "xb", [S, H])
        delta = sb(att, "delta", [S, H])
        x1 = sb(att, "x1", [S, H])
        xn = sb(att, "xn", [S, H])
        stats_b = sb(att, "stats_b", [S, 2, 6])
        mv = sb(att, "mv", [S, 2, 2])
        rs_b = sb(att, "rs_b", [S, 6])
        xn_p = sb(att, "xn_p", [P, 2, KT, S], fp32r)
        x1_t = sb(att, "x1_t", [P, KT, S])

        ctx_loaded = sem("ctx_loaded")
        q_loaded = sem("q_loaded")
        x_loaded = [sem(f"x_loaded{i}") for i in range(2)]
        idx_loaded = sem("idx_loaded")
        zeroed = sem("zeroed")
        ctx_hi = sem("ctx_hi")
        ctx_lo = sem("ctx_lo")
        k_mm = sem("k_mm")
        k_hi = sem("k_hi")
        k_lo = sem("k_lo")
        v_mm = sem("v_mm")
        v_copied = sem("v_copied")
        scores_done = sem("scores_done")
        exp_done = sem("exp_done")
        clip_done = sem("clip_done")
        pv_done = sem("pv_done")
        den_done = sem("den_done")
        divided = sem("divided")
        att_hi = sem("att_hi")
        att_lo = sem("att_lo")
        o_mm = sem("o_mm")
        ln_dve = sem("ln_dve")
        ln_pool = sem("ln_pool")
        xb_done = sem("xb_done")
        xn_tr = sem("xn_tr")
        xn_hi = sem("xn_hi")
        xn_lo = sem("xn_lo")
        x1_tr = sem("x1_tr")
        x1_copied = sem("x1_copied")
        rows_stored = sem("rows_stored")
        inverted = sem("inverted")

        def by_pair(half, row, u):
            return pv_ps[half][row:row + HD, 0:4 * S].rearrange("p (g u s) -> p g u s", g=2, u=2)[:, :, u, :]

        LN = 7
        LNP = 7
        R0 = len(PRE)
        N0 = LPRE

        def live(b):
            return not isinstance(b, int) or 0 <= b < B

        def all_iterations(engine, iteration):
            for b in range(-1, 3):
                iteration(b, b % 2)
            with engine.Fori(3, B - 4, 2) as i:
                iteration(i, 1)
                iteration(i + 1, 0)
            for b in range(B - 3, B + 2):
                iteration(b, b % 2)

        with nc.Block() as block:
            @block.tensor
            def _(pe):
                def parts(out, left, right, n_of):
                    todo = [(a, b, k) for a, b in ((0, 0), (0, 1), (1, 0)) for k in range(KT)]
                    for n, (a, b, k) in enumerate(todo):
                        mm = nc.tensor.matmul(out, left(a, k), right(b, k), start=(n == 0), stop=(n == len(todo) - 1))
                        if n == len(todo) // 2 - 1:
                            yield mm
                    mm.then_inc(n_of, 1)
                    yield mm

                def k_unit(n, s, m):
                    if m == 0:
                        pe.wait_ge(ctx_lo, n + 1)
                        if isinstance(n, int) and n == 0:
                            pe.wait_ge(zeroed, 4)
                        if isinstance(n, int) and n < 3:
                            need(pe, k_lo, NG * (n - 1) + 3)
                        else:
                            pe.wait_ge(ln_dve, LN * (n - 3) + 1)
                    elif m == 1:
                        need(pe, v_copied, TT * n)
                    else:
                        pe.wait_ge(k_lo, NG * n + m - 1)
                    bank = work[(m + 1) % 2]
                    return parts(bank[:, 0:TE], lambda a, k: wk[a][:, k, m * P:(m + 1) * P],
                                 lambda b, k: ctx_t[s][b][:, k, :], k_mm)

                def v_unit(n, s, t):
                    if t == 0:
                        pe.wait_ge(k_lo, NG * n + 4)
                    else:
                        pe.wait_ge(v_copied, TT * n + t)
                    return parts(work[0][0:TP, :], lambda a, k: ctx_t[s][a][:, k, t * TP:(t + 1) * TP],
                                 lambda b, k: wv[b][:, k, :], v_mm)

                def out_proj(b):
                    pe.wait_ge(att_lo, b + 1)
                    if isinstance(b, int) and b == 0:
                        pe.wait_ge(k_lo, NG * 2 + 3)
                    else:
                        pe.wait_ge(x1_copied, b)
                    for _ in parts(work[1][0:S, :], lambda a, k: att_p[a][:, k, :], lambda c, k: wo[c][:, k, :], o_mm):
                        pass

                def transposed(src, done):
                    for k in range(KT):
                        mm = nc.tensor.transpose(work[1][:, k * S:(k + 1) * S], src[:, k * P:(k + 1) * P],
                                                 ident[0:S, 0:S])
                    mm.then_inc(done, 1)

                def transpose_xn(b):
                    pe.wait_ge(ln_dve, LN * (b + 1))
                    if live(b + 3):
                        pe.wait_ge(k_lo, NG * (b + 3) + 3)
                    transposed(xn, xn_tr)

                def transpose_x1(b):
                    pe.wait_ge(xn_lo, b + 1)
                    transposed(x1, x1_tr)

                def scores(b, s, g, t):
                    i = TT * g + t
                    if i == 0:
                        pe.wait_ge(q_loaded, 64 * (b + 1))
                    if t == 0:
                        pe.wait_ge(k_lo, NG * b + g + 1)
                    need(pe, exp_done, TT * NG * b + i - 1)
                    for n, (a, c) in enumerate(((0, 0), (0, 1), (1, 0))):
                        mm = nc.tensor.matmul(score_ps[i % 2][0:TP, 0:GC], k_t[s][a][:, g, t * TP:(t + 1) * TP],
                                              q_blk[:, c, g, :], start=(n == 0), stop=(n == 2))
                    mm.then_inc(scores_done, 1)

                def pv(b, s, g):
                    pe.wait_ge(clip_done, TT * (NG * b + g + 1))
                    if g == 0:
                        pe.wait_ge(v_copied, TT * (b + 1))
                    if g % 2 == 0:
                        need(pe, divided, 4 * (2 * b + g // 2 - 1))
                    for u in range(2):
                        for t in range(TT):
                            for odd in range(2):
                                j = 2 * u + odd
                                h = HG * g + j
                                col = ((g % 2) * 2 + u) * S
                                mm = nc.tensor.matmul(pv_ps[g // 2][64 * odd:64 * odd + 64, col:col + S],
                                                      val[s][:, t, h // 2, odd:odd + 2, :],
                                                      prob[g % 2][:, t, j * S:(j + 1) * S],
                                                      start=(t == 0), stop=(t == TT - 1))
                    mm.then_inc(pv_done, 1)

                def iteration(b, s):
                    def project():
                        for m in range(NG):
                            yield from k_unit(b + 1, 1 - s, m)
                        for t in range(TT):
                            yield from v_unit(b + 1, 1 - s, t)
                    halves = project() if live(b + 1) else None

                    def half():
                        if halves:
                            next(halves)

                    def sc(g, t):
                        if live(b):
                            scores(b, s, g, t)

                    def out(g):
                        if live(b):
                            pv(b, s, g)
                    sc(0, 0); half(); sc(0, 1); half(); sc(0, 2)
                    sc(1, 0); half(); sc(1, 1); half(); sc(1, 2)
                    out(0); half()
                    sc(2, 0); half(); sc(2, 1); half(); sc(2, 2)
                    out(1); half()
                    if live(b - 2):
                        transpose_xn(b - 2)
                    sc(3, 0); half(); sc(3, 1); half(); sc(3, 2)
                    out(2)
                    if live(b - 2):
                        transpose_x1(b - 2)
                    half()
                    if live(b - 1):
                        out_proj(b - 1)
                    half()
                    out(3); half(); half()

                all_iterations(pe, iteration)

            @block.scalar
            def _(act):
                def split_ctx(n, s):
                    act.wait_ge(ctx_loaded, 16 * (n + 1))
                    need(act, v_mm, TT * (n - 1))
                    nc.scalar.activation(ctx_t[s][0][:, :, 0:T], ctx_in[:], ACT.Copy).then_inc(ctx_hi, 1)

                def key_hi(n, s, m):
                    act.wait_ge(k_mm, NG * n + m + 1)
                    if m == 0:
                        need(act, scores_done, TT * NG * (n - 1))
                    nc.scalar.activation(k_t[s][0][:, m, :], work[(m + 1) % 2][:, 0:TE], ACT.Identity,
                                         bias=bk[:, m:m + 1]).then_inc(k_hi, 1)

                def value(n, s, t):
                    act.wait_ge(v_mm, TT * n + t + 1)
                    if t == 0:
                        need(act, pv_done, NG * (n - 1))
                        if isinstance(n, int) and n < 2:
                            act.wait_ge(zeroed, 6)
                    nc.scalar.activation(val[s][:, t, :, 0:3:2, :], work[0][0:TP, :].rearrange(
                        "p (h o d) -> p h o d", o=2, d=HD), ACT.Copy).then_inc(v_copied, 1)

                def exp(b, g, t):
                    i = TT * g + t
                    act.wait_ge(scores_done, TT * NG * b + i + 1)
                    if t == 0:
                        need(act, pv_done, NG * b + g - 1)
                    nc.scalar.activation(prob[g % 2][:, t, :], score_ps[i % 2][0:TP, 0:GC], ACT.Exp,
                                         scale=SCORE_SCALE).then_inc(exp_done, 1)

                def sums(b, half):
                    act.wait_ge(pv_done, NG * b + 2 * half + 2)
                    need(act, divided, 4 * (2 * b + half - 1))
                    for odd in range(2):
                        for u in range(2):
                            q = HD * (2 * odd + u)
                            nc.scalar.activation(den[half][q:q + HD, :, :], by_pair(half, 32 + 32 * odd, u), ACT.Copy,
                                                 scale=1.0 + EPS_PROBS).then_inc(den_done, 1)

                def att_high(b):
                    act.wait_ge(divided, 8 * (b + 1))
                    need(act, o_mm, b)
                    nc.scalar.activation(att_p[0][:], att_t[:], ACT.Copy).then_inc(att_hi, 1)

                def xn_high(b):
                    act.wait_ge(xn_tr, b + 1)
                    need(act, rows_stored, 32 * b)
                    nc.scalar.activation(xn_p[:, 0, :, :], work[1][:, 0:KT * S].rearrange("p (k s) -> p k s", k=KT),
                                         ACT.Copy).then_inc(xn_hi, 1)

                def x1_copy(b):
                    act.wait_ge(x1_tr, b + 1)
                    nc.scalar.activation(x1_t[:], work[1][:, 0:KT * S].rearrange("p (k s) -> p k s", k=KT),
                                         ACT.Copy).then_inc(x1_copied, 1)

                def iteration(b, s):
                    steps = iter([(R0 + b, N0 + LB * b + k, k, LP, j) for k in range(LB) for j in range(NPAIR)])

                    def ex(g, t):
                        if live(b):
                            exp(b, g, t)

                    def look():
                        if live(b):
                            lookup_pair(act, *next(steps))

                    def kh(m):
                        if live(b + 1):
                            key_hi(b + 1, 1 - s, m)

                    def va(t):
                        if live(b + 1):
                            value(b + 1, 1 - s, t)
                    ex(0, 0)
                    if live(b - 1):
                        sums(b - 1, 1)
                    look(); ex(0, 1); look(); kh(0); ex(0, 2); look()
                    ex(1, 0); look()
                    if live(b - 1):
                        att_high(b - 1)
                    ex(1, 1); look(); kh(1); ex(1, 2); look()
                    if live(b + 2):
                        split_ctx(b + 2, s)
                    ex(2, 0); look(); kh(2); ex(2, 1); look(); ex(2, 2); look()
                    if live(b):
                        sums(b, 0)
                    kh(3)
                    ex(3, 0)
                    if live(b - 2):
                        xn_high(b - 2)
                    look(); ex(3, 1); look(); va(0); ex(3, 2); look(); look()
                    if live(b - 2):
                        x1_copy(b - 2)
                    look(); va(1)
                    if live(b):
                        lookup_hi(act, R0 + b, N0 + LB * b, 0, LP)
                    look(); va(2); look()
                    if live(b):
                        lookup_hi(act, R0 + b, N0 + LB * b + 1, 1, LP)

                split_ctx(0, 0)
                all_iterations(act, iteration)

            @block.vector
            def _(dve):
                for s in range(2):
                    for i in range(2):
                        nc.vector.memset(ctx_t[s][i][:, :, T:TE].bitcast(fp32), 0.0).then_inc(zeroed, 1)
                for s in range(2):
                    nc.vector.memset(val[s][:, :, :, 1, :], 1.0).then_inc(zeroed, 1)
                nc.vector.memset(q_blk[:].bitcast(fp32), 0.0).then_inc(zeroed, 1)

                def clip(b, g, t):
                    dve.wait_ge(exp_done, TT * (NG * b + g) + t + 1)
                    p_ = prob[g % 2][:, t, :]
                    nc.vector.tensor_scalar(p_, p_, CLIP_LO, prob_cap[:, t, bass.ds(b, 1)], ALU.max, ALU.min)\
                        .then_inc(clip_done, 1)

                def key_lo(n, s, m):
                    dve.wait_ge(k_hi, NG * n + m + 1)
                    nc.vector.scalar_tensor_tensor(k_t[s][1][:, m, :], work[(m + 1) % 2][:, 0:TE],
                                                   bk[:, m:m + 1], k_t[s][0][:, m, :], ALU.add, ALU.subtract)\
                        .then_inc(k_lo, 1)

                def divide(b, half):
                    dve.wait_ge(den_done, 4 * (2 * b + half + 1))
                    nc.vector.reciprocal(den[half][:], den[half][:]).then_inc(inverted, 1)
                    dve.wait_ge(inverted, 2 * b + half + 1)
                    need(dve, att_lo, b)
                    for odd in range(2):
                        for u in range(2):
                            q = HD * (2 * odd + u)
                            nc.vector.tensor_tensor(att_t[q:q + HD, 2 * half:2 * half + 2, :],
                                                    by_pair(half, 96 * odd, u), den[half][q:q + HD, :, :],
                                                    ALU.mult).then_inc(divided, 1)

                def ln(b, k):
                    done = LN * b
                    if k == 0:
                        dve.wait_ge(o_mm, b + 1)
                        need(dve, ln_pool, LNP * (b - 1) + 5)
                        nc.vector.tensor_tensor(delta[:], work[1][0:S, :], bo[0:S, :], ALU.add).then_inc(ln_dve, 1)
                    elif k == 1:
                        need_apart(dve, ln_dve, done + 1)
                        nc.vector.bn_stats(stats_b[:, 0, :], delta[:]).then_inc(ln_dve, 1)
                    elif k == 2:
                        need_apart(dve, ln_dve, done + 2)
                        nc.vector.bn_aggr(mv[:, 0, :], stats_b[:, 0, :]).then_inc(ln_dve, 1)
                    elif k == 3:
                        dve.wait_ge(ln_pool, LNP * b + 3)
                        nc.vector.tensor_scalar(delta[:], delta[:], mv[:, 0, 0:1], rs_b[:, 2:3], ALU.subtract, ALU.mult)\
                            .then_inc(ln_dve, 1)
                    elif k == 4:
                        need_apart(dve, ln_pool, LNP * b + 5)
                        nc.vector.bn_stats(stats_b[:, 1, :], x1[:]).then_inc(ln_dve, 1)
                    elif k == 5:
                        need_apart(dve, ln_dve, done + 5)
                        nc.vector.bn_aggr(mv[:, 1, :], stats_b[:, 1, :]).then_inc(ln_dve, 1)
                    else:
                        dve.wait_ge(ln_pool, LNP * b + 7)
                        need(dve, xn_tr, b)
                        nc.vector.tensor_scalar(xn[:], x1[:], mv[:, 1, 0:1], rs_b[:, 4:5], ALU.subtract, ALU.mult)\
                            .then_inc(ln_dve, 1)

                def xn_low(b):
                    dve.wait_ge(xn_hi, b + 1)
                    nc.vector.tensor_tensor(xn_p[:, 1, :, :], work[1][:, 0:KT * S].rearrange("p (k s) -> p k s", k=KT),
                                            xn_p[:, 0, :, :], ALU.subtract).then_inc(xn_lo, 1)

                def iteration(b, s):
                    steps = iter([(R0 + b, N0 + LB * b + k, k, LP, j) for k in range(LB) for j in range(1, NPAIR)])

                    def cl(g, t):
                        if live(b):
                            clip(b, g, t)

                    def kl(m):
                        if live(b + 1):
                            key_lo(b + 1, 1 - s, m)

                    def look():
                        if live(b):
                            lookup_pick(dve, *next(steps))

                    def lns(b, *ks):
                        if live(b):
                            for k in ks:
                                ln(b, k)
                    cl(0, 0)
                    if live(b - 1):
                        divide(b - 1, 1)
                    cl(0, 1); lns(b - 2, 3); kl(0); cl(0, 2); look()
                    cl(1, 0); look(); cl(1, 1); look(); kl(1); cl(1, 2); lns(b - 2, 4, 5); look()
                    cl(2, 0); look(); kl(2); cl(2, 1); look(); lns(b - 2, 6); cl(2, 2); look(); kl(3)
                    if live(b):
                        divide(b, 0)
                    cl(3, 0); look()
                    if live(b - 2):
                        xn_low(b - 2)
                    cl(3, 1); look(); cl(3, 2); look(); look()
                    lns(b - 1, 0); look(); lns(b - 1, 1); look(); lns(b - 1, 2); look()
                    if live(b + 1):
                        next_masks(b + 1)

                def next_masks(b):
                    dve.wait_ge(idx_loaded, 16 * (b + 1))
                    lookup_masks(dve, R0 + b, N0 + LB * b, LW)

                all_iterations(dve, iteration)

            @block.gpsimd
            def _(pool):
                def split_ctx(n, s):
                    pool.wait_ge(ctx_hi, n + 1)
                    nc.gpsimd.tensor_tensor(ctx_t[s][1][:, :, 0:T], ctx_in[:], ctx_t[s][0][:, :, 0:T], ALU.subtract)\
                        .then_inc(ctx_lo, 1)

                def add_beta(b, s):
                    pool.wait_ge(x_loaded[s], 16 * ((b + 2 - s) // 2) if isinstance(b, int) else 8 * (b + 2 - s))
                    need(pool, ln_pool, LNP * (b - 1) + 5)
                    nc.gpsimd.tensor_tensor(xb[:], xr[s][:], beta[0:S, :], ALU.add).then_inc(xb_done, 1)

                def att_low(b):
                    pool.wait_ge(att_hi, b + 1)
                    nc.gpsimd.tensor_tensor(att_p[1][:], att_t[:], att_p[0][:], ALU.subtract).then_inc(att_lo, 1)

                def ln(b, k):
                    done = LNP * b
                    if k == 0:
                        need_apart(pool, ln_dve, LN * b + 3)
                        nc.gpsimd.tensor_scalar(rs_b[:, 0:1], mv[:, 0, 1:2], res[0:S, 1:2], EPS_LN, ALU.mult, ALU.add)\
                            .then_inc(ln_pool, 1)
                    elif k == 1:
                        pool.wait_ge(ln_pool, done + 1)
                        nc.gpsimd.tensor_tensor(rs_b[:, 1:2], rs_b[:, 0:1], neg_half[0:S, 0:1], ALU.pow)\
                            .then_inc(ln_pool, 1)
                    elif k == 2:
                        pool.wait_ge(ln_pool, done + 2)
                        nc.gpsimd.tensor_tensor(rs_b[:, 2:3], rs_b[:, 1:2], res[0:S, 0:1], ALU.mult).then_inc(ln_pool, 1)
                    elif k == 3:
                        pool.wait_ge(ln_dve, LN * b + 4)
                        nc.gpsimd.tensor_tensor(delta[:], delta[:], gamma[0:S, :], ALU.mult).then_inc(ln_pool, 1)
                    elif k == 4:
                        pool.wait_ge(ln_pool, done + 4)
                        pool.wait_ge(xb_done, b + 1)
                        need(pool, x1_tr, b)
                        nc.gpsimd.tensor_tensor(x1[:], delta[:], xb[:], ALU.add).then_inc(ln_pool, 1)
                    elif k == 5:
                        need_apart(pool, ln_dve, LN * b + 6)
                        nc.gpsimd.tensor_scalar(rs_b[:, 3:4], mv[:, 1, 1:2], EPS_LN, 1.0, ALU.add, ALU.mult)\
                            .then_inc(ln_pool, 1)
                    else:
                        pool.wait_ge(ln_pool, done + 6)
                        nc.gpsimd.tensor_tensor(rs_b[:, 4:5], rs_b[:, 3:4], neg_half[0:S, 0:1], ALU.pow)\
                            .then_inc(ln_pool, 1)

                def iteration(b, s):
                    def lns(b, *ks):
                        if live(b):
                            for k in ks:
                                ln(b, k)
                    lns(b - 2, 3, 4)
                    if live(b - 1):
                        att_low(b - 1)
                        add_beta(b - 1, 1 - s)
                    lns(b - 2, 5, 6)
                    if live(b + 2):
                        split_ctx(b + 2, s)
                    if live(b):
                        lookup_lo(pool, N0 + LB * b, 0, LP)
                    lns(b - 1, 0, 1, 2)
                    if live(b):
                        lookup_lo(pool, N0 + LB * b + 1, 1, LP)

                split_ctx(0, 0)
                all_iterations(pool, iteration)

            @block.sync
            def _(sp):
                def load_ctx(n):
                    need(sp, ctx_lo, n)
                    sp.dma_start(ctx_in[:], ins["ctx"][n]).then_inc(ctx_loaded, 16)

                def load_q(b):
                    need(sp, scores_done, TT * NG * b)
                    for j in range(HG):
                        sp.dma_start(q_blk[j * HD:(j + 1) * HD, :, :, j * S:(j + 1) * S].bitcast(fp32),
                                     q_dram[j * HD:(j + 1) * HD, :, :, bass.ds(b * S, S)]).then_inc(q_loaded, 16)

                def load_x(b, s):
                    need(sp, xb_done, b - 1)
                    sp.dma_start(xr[s][:], ins["x"][bass.ds(b * S, S), :]).then_inc(x_loaded[s], 16)

                def load_idx(b):
                    sp.wait_ge(bits_done, 2 * (R0 + b))
                    sp.dma_start(idx[:], ins["idx"][:, bass.ds(b * LW, LW)]).then_inc(idx_loaded, 16)

                def store_rows(b):
                    sp.wait_ge(xn_lo, b + 1)
                    sp.dma_start(xn_dram[:, :, :, bass.ds(b * S, S)].rearrange("p a k s -> p (a k) s"),
                                 xn_p[:].rearrange("p a k s -> p (a k) s").bitcast(fp32)).then_inc(rows_stored, 16)
                    sp.wait_ge(x1_copied, b + 1)
                    sp.dma_start(x1_dram[:, :, bass.ds(b * S, S)], x1_t[:]).then_inc(rows_stored, 16)

                def iteration(b, s):
                    if live(b + 3):
                        load_ctx(b + 3)
                    if live(b + 1) and live(b):
                        load_idx(b + 1)
                        load_q(b + 1)
                        load_x(b + 1, 1 - s)
                    if live(b - 2):
                        store_rows(b - 2)
                    if live(b):
                        for k in range(LB):
                            lookup_store(sp, N0 + LB * b + k, k, LP, b * LW + k * LP)

                load_ctx(0)
                sp.wait_ge(zeroed, 7)
                load_q(0)
                load_idx(0)
                load_x(0, 0)
                load_ctx(1)
                all_iterations(sp, iteration)
                for k in range(LB):
                    sp.wait_ge(w_stored[k], 32 * (R0 + B))
                sp.wait_ge(rows_stored, 32 * B)
        att.close()

        ffn = ExitStack()
        wf = [sb(ffn, f"wf{i}", [P, WCOLS], fp32r) for i in range(2)]
        xf = [sb(ffn, f"xf{s}", [P, 2, KT, CH], fp32r) for s in range(2)]
        x1f = [sb(ffn, f"x1f{s}", [P, KT, CH]) for s in range(2)]
        silu = [sb(ffn, f"silu{s}", [P, CH]) for s in range(2)]
        hid = [sb(ffn, f"hid{s}", [P, CH]) for s in range(2)]
        hid_p = [[sb(ffn, f"hid_p{s}{i}", [P, CH], fp32r) for i in range(2)] for s in range(2)]

        wf_loaded = [sem(f"wf_loaded{j}") for j in range(JT)]
        xf_loaded = [sem(f"xf_loaded{s}") for s in range(2)]
        gate_mm = sem("gate_mm")
        up_mm = sem("up_mm")
        silu_done = sem("silu_done")
        hid_done = sem("hid_done")
        hid_hi = sem("hid_hi")
        hid_lo = sem("hid_lo")
        down_mm = sem("down_mm")
        down_all = sem("down_all")
        y_done = sem("y_done")
        y_stored = [sem(f"y_stored{s}") for s in range(2)]
        gate_ps, up_ps = work, score_ps
        acc = pv_ps + pair_ps
        PARTS = ((0, 0), (0, 1), (1, 0))
        FREE = 2

        def gate_w(a, j, k):
            return wf[a][:, JCOL[j] + k * JW[j]:JCOL[j] + (k + 1) * JW[j]]

        def up_w(a, j, k):
            return wf[a][:, JCOL[j] + (KT + k) * JW[j]:JCOL[j] + (KT + k + 1) * JW[j]]

        def down_w(a, j, m):
            at = JCOL[j] + 2 * KT * JW[j] + m * P
            return wf[a][0:JW[j], at:at + P]

        with nc.Block() as block:
            @block.sync
            def _(sp):
                def load_rows(c, s):
                    sp.dma_start(xf[s][:].rearrange("p a k s -> p (a k) s").bitcast(fp32),
                                 xn_dram[:, :, :, bass.ds(c * CH, CH)].rearrange("p a k s -> p (a k) s"))\
                        .then_inc(xf_loaded[s], 16)
                    sp.dma_start(x1f[s][:], x1_dram[:, :, bass.ds(c * CH, CH)]).then_inc(xf_loaded[s], 16)
                load_rows(0, 0)
                for j in range(JT):
                    end = JCOL[j + 1] if j + 1 < JT else WCOLS
                    for a in range(2):
                        sp.dma_start(wf[a][:, JCOL[j]:end].bitcast(fp32), w_dram[:, a, JCOL[j]:end]).then_inc(wf_loaded[j], 16)
                    if j == 1:
                        load_rows(1, 1)
                for c in range(NC):
                    s = c % 2
                    sp.wait_ge(y_done, KT * (c + 2))
                    sp.dma_start(out_t[:, :, c * CH:(c + 1) * CH].rearrange("k p s -> p k s"), x1f[s][:])\
                        .then_inc(y_stored[s], 16)
                    if c + 2 < NC:
                        sp.wait_ge(y_stored[s], 16 * (c // 2 + 1))
                        load_rows(c + 2, s)
                for s in range(2):
                    sp.wait_ge(y_stored[s], 16 * NC // 2)

            @block.tensor
            def _(pe):
                def up_units(c, s, j):
                    w = JW[j]
                    if j == 0:
                        pe.wait_ge(xf_loaded[s], 16 * (c + 2 - s))
                    pe.wait_ge(wf_loaded[j], 32)
                    for name, bank, wts, n_of, free, at in (
                            ("gate", gate_ps, gate_w, gate_mm, silu_done, JT * c + j - (j > 0) + FREE),
                            ("up", up_ps, up_w, up_mm, hid_done, JT * c + j - (j > 0) + FREE)):
                        pe.wait_ge(free, at)
                        for n, (a, b) in enumerate(PARTS):
                            for k in range(KT):
                                mm = nc.tensor.matmul(bank[j % 2][0:w, 0:CH], wts(a, j, k), xf[s][:, b, k, :],
                                                      start=(n == 0 and k == 0), stop=(n == 2 and k == KT - 1))
                        mm.then_inc(n_of, 1)

                def down_units(c, s, j):
                    w = JW[j]
                    pe.wait_ge(hid_lo, JT * c + j + 1 + FREE)
                    if j == 0:
                        pe.wait_ge(y_done, KT * (c + 1))
                    for m in range(KT):
                        for n, (a, b) in enumerate(PARTS):
                            mm = nc.tensor.matmul(acc[m][:, 0:CH], down_w(a, j, m), hid_p[j % 2][b][0:w, :],
                                                  start=(j == 0 and n == 0), stop=(j == JT - 1 and n == 2))
                    mm.then_inc(down_mm, 1)

                def chunk(c, s):
                    for j in range(JT):
                        up_units(c, s, j)
                        if j > 0:
                            down_units(c, s, j - 1)
                    down_units(c, s, JT - 1)

                pe.sem_inc(down_mm, FREE)
                with pe.Fori(0, NC - 1, 2) as c:
                    chunk(c, 0)
                    chunk(c + 1, 1)

            @block.scalar
            def _(act):
                def silu_of(c, j):
                    w = JW[j]
                    act.wait_ge(gate_mm, JT * c + j + 1)
                    act.wait_ge(hid_done, JT * c + j - (j > 0) + FREE)
                    nc.scalar.activation(silu[j % 2][0:w, :], gate_ps[j % 2][0:w, 0:CH], ACT.Silu).then_inc(silu_done, 1)

                def high_of(c, j):
                    w = JW[j]
                    act.wait_ge(hid_done, JT * c + j + 1 + FREE)
                    act.wait_ge(down_mm, JT * c + j - (j > 0) + FREE)
                    nc.scalar.activation(hid_p[j % 2][0][0:w, :], hid[j % 2][0:w, :], ACT.Copy).then_inc(hid_hi, 1)

                act.sem_inc(silu_done, FREE)
                with act.Fori(0, NC, 1) as c:
                    for j in range(JT):
                        silu_of(c, j)
                        high_of(c, j)

            @block.vector
            def _(dve):
                def chunk(c, s):
                    for j in range(JT):
                        w = JW[j]
                        dve.wait_ge(silu_done, JT * c + j + 1 + FREE)
                        dve.wait_ge(up_mm, JT * c + j + 1)
                        dve.wait_ge(hid_lo, JT * c + j - (j > 0) + FREE)
                        nc.vector.tensor_tensor(hid[j % 2][0:w, :], silu[j % 2][0:w, :], up_ps[j % 2][0:w, 0:CH],
                                                ALU.mult).then_inc(hid_done, 1)
                        dve.wait_ge(hid_hi, JT * c + j + 1)
                        nc.vector.tensor_tensor(hid_p[j % 2][1][0:w, :], hid[j % 2][0:w, :], hid_p[j % 2][0][0:w, :],
                                                ALU.subtract).then_inc(hid_lo, 1)
                    dve.wait_ge(down_mm, JT * (c + 1) + FREE)
                    for m in range(KT):
                        nc.vector.scalar_tensor_tensor(x1f[s][:, m, :], acc[m][:, 0:CH], tanh_g[:, 1:2], x1f[s][:, m, :],
                                                       ALU.mult, ALU.add).then_inc(y_done, 1)
                dve.sem_inc(hid_done, FREE)
                dve.sem_inc(hid_lo, FREE)
                dve.sem_inc(y_done, KT)
                with dve.Fori(0, NC - 1, 2) as c:
                    chunk(c, 0)
                    chunk(c + 1, 1)
        ffn.close()


def kernel(**inputs):
    import numpy as np
    import concourse.bacc as bacc
    from concourse import mybir as mb
    from concourse.bass_utils import run_bass_kernel_spmd

    a = {k: np.asarray(v) for k, v in inputs.items()}
    quad = [0, 2, 1, 3]
    order = np.concatenate([np.arange(HD) + HD * (HG * g + quad[q]) for g in range(NG) for q in range(HG)])

    def rows(v):
        return np.ascontiguousarray(np.broadcast_to(v.reshape(1, -1), (P, v.size)))

    def feature_major(w):
        return np.ascontiguousarray(w.T.reshape(KT, P, -1).transpose(1, 0, 2))

    def columns(v):
        return np.ascontiguousarray(v.reshape(KT, P).T)

    gate, up, down = (a["L0_ffn_" + n] for n in ("gate_idx", "up_idx", "down_idx"))
    gate_f, up_f = feature_major(gate), feature_major(up)
    blocks = []
    for j in range(JT):
        cols = slice(j * P, j * P + JW[j])
        blocks += [gate_f[:, :, cols].reshape(P, -1), up_f[:, :, cols].reshape(P, -1)]
        tile = np.zeros((P, H), down.dtype)
        tile[:JW[j]] = down.T[cols]
        blocks.append(tile)
    arrays = {
        "x": np.ascontiguousarray(a["x"].reshape(ROWS, H)),
        "x4": np.ascontiguousarray(a["x"].reshape(NC, CB, S, H).transpose(0, 2, 1, 3)),
        "ctx": np.ascontiguousarray(a["ctx_2048"].reshape(B, T, KT, P).transpose(0, 3, 2, 1)),
        "mask": np.ascontiguousarray(a["mask_BxS2_ik0"].reshape(B, TT, TP).transpose(2, 1, 0)),
        "wq": feature_major(a["L0_xattn_Wq"]),
        "wk": feature_major(a["L0_xattn_Wk"]),
        "wv": feature_major(a["L0_xattn_Wv"]),
        "wo": feature_major(a["L0_xattn_Wo"][:, order]),
        "bq": columns(a["L0_xattn_bq"]),
        "bk": columns(a["L0_xattn_bk"]),
        "bv": columns(a["L0_xattn_bv"][order]),
        "bo": rows(a["L0_xattn_bo"]),
        "gamma": rows(a["L0_xattn_ln_gamma"]),
        "beta": rows(a["L0_xattn_ln_beta"]),
        "lut": rows(a["L0_ffn_lut"]),
        "g_xattn": rows(a["g_xattn"]),
        "g_ffn": rows(a["g_ffn"]),
        "res": rows(a["L0_xattn_residual_scale"].reshape(1)),
        "idx": np.ascontiguousarray(np.concatenate(blocks, axis=1)),
    }
    nc = bacc.Bacc("TRN2", target_bir_lowering=False, num_devices=1)
    ins = {n: nc.dram_tensor(f"in_{n}", v.shape, mb.dt.from_np(v.dtype), kind="ExternalInput").ap()
           for n, v in arrays.items()}
    out_t = nc.dram_tensor("out_t", (KT, P, ROWS), mb.dt.float32, kind="ExternalOutput").ap()
    flamingo_kernel(nc, ins, out_t)
    r = run_bass_kernel_spmd(nc, [{f"in_{n}": v for n, v in arrays.items()}], core_ids=[0])
    got = r.results[0]["out_t"]
    return np.ascontiguousarray(got.reshape(H, ROWS).T).reshape(B, S, H)
```

```python
from contextlib import ExitStack

import concourse.bass as bass
from concourse import mybir

B, S, T, H, NH = 16, 112, 375, 512, 16
INTER = 1376
P = 128
HD = H // NH
KT = H // P
HG = P // HD
NG = NH // HG
TT = 3
TP = T // TT
TE = T + 1
ROWS = B * S
CB = 4
NC = B // CB
CH = CB * S
GC = HG * S
JT = -(-INTER // P)
JW = [min(P, INTER - j * P) for j in range(JT)]
JCOL = [j * (2 * KT * P + H) for j in range(JT)]
WCOLS = JCOL[-1] + 2 * KT * JW[-1] + H
LATE = 1
LATE_COL = JCOL[JT - LATE]
LB = 2
LP = LATE_COL // (B * LB)
LW = LB * LP
assert LW * B == LATE_COL
LATE_LP = 320
LATE_PIECES = [(n, LATE_COL + n * LATE_LP, min(LATE_LP, WCOLS - LATE_COL - n * LATE_LP))
               for n in range(-(-(WCOLS - LATE_COL) // LATE_LP))]
LUT = 16
NPAIR = LUT // 2
PICKS = NPAIR - 1
MASK_BITS = 14
EPS_LN = 1e-5
EPS_PROBS = 1e-8
SCORE_SCALE = HD ** -0.5
CLIP_HI = float(2.718281828459045 ** 50.0)
CLIP_LO = float(2.718281828459045 ** -50.0)
RES_MAX = 0.3


def flamingo_kernel(nc, ins, out_t):
    fp32, fp32r = mybir.dt.float32, mybir.dt.float32r
    i32, u16 = mybir.dt.int32, mybir.dt.uint16
    ALU = mybir.AluOpType
    ACT = mybir.ActivationFunctionType

    def need(engine, sem, value):
        if isinstance(value, int) and value <= 0:
            return
        assert isinstance(value, int) or value.min_val > 0
        engine.wait_ge(sem, value)

    def need_apart(engine, sem, value):
        need(engine, sem, value)
        engine.nop(nofuse=True)

    q_dram = nc.dram_tensor("q_parts", (P, 2, NG, ROWS), fp32, kind="Internal").ap()
    w_dram = nc.dram_tensor("w_parts", (P, 2, WCOLS), fp32, kind="Internal").ap()
    xn_dram = nc.dram_tensor("xn_parts", (P, 2, KT, ROWS), fp32, kind="Internal").ap()
    x1_dram = nc.dram_tensor("x1_rows_t", (P, KT, ROWS), fp32, kind="Internal").ap()

    top = ExitStack()
    with top:
        def sb(stack, name, shape, dt=fp32):
            return stack.enter_context(nc.sbuf_tensor(name, shape, dt))

        def ps(stack, name, shape, dt=fp32):
            return stack.enter_context(nc.psum_tensor(name, shape, dt))

        def sem(name):
            return top.enter_context(nc.semaphore(name))

        work = [ps(top, f"work{i}", [P, 512]) for i in range(2)]
        score_ps = [ps(top, f"score_ps{i}", [P, 512]) for i in range(2)]
        pv_ps = [ps(top, f"pv_ps{i}", [P, 512]) for i in range(2)]
        pair_ps = [ps(top, f"pair_ps{i}", [P, 512]) for i in range(2)]

        ident = sb(top, "ident", [P, P])
        neg_half = sb(top, "neg_half", [P, CB])
        lut = sb(top, "lut", [P, LUT])
        lut_step = sb(top, "lut_step", [P, NPAIR])
        gates = sb(top, "gates", [P, 2])
        tanh_g = sb(top, "tanh_g", [P, 2])
        res = sb(top, "res", [P, 2])

        CT = KT * TE
        ROW_COLS = 2 * KT * CH
        TILE = JCOL[1]
        early = sb(top, "early", [P, max(4 * CT, 2 * ROW_COLS)], fp32r)
        ctx_t = [[early[:, (2 * s + i) * CT:(2 * s + i + 1) * CT].rearrange("p (k t) -> p k t", k=KT)
                  for i in range(2)] for s in range(2)]
        xf = early[:, 0:2 * ROW_COLS].rearrange("p (c a k s) -> p c a k s", c=2, a=2, k=KT)
        wk = [sb(top, f"wk{i}", [P, KT, H], fp32r) for i in range(2)]
        wv = [sb(top, f"wv{i}", [P, KT, H], fp32r) for i in range(2)]
        flat = [[w[i][:].rearrange("p k h -> p (k h)") for i in range(2)] for w in (wk, wv)]
        w_early = [[flat[j][a][:, 0:TILE] for a in range(2)] for j in range(2)]
        hid_p = [[flat[s][i][:, TILE:TILE + CH] for i in range(2)] for s in range(2)]
        assert TILE + CH <= KT * H

        xn_p = sb(top, "xn_p", [P, 2, KT, S], fp32r)
        x1_t = sb(top, "x1_t", [P, KT, S])

        att = ExitStack()
        wo = [sb(att, f"wo{i}", [P, KT, H], fp32r) for i in range(2)]
        ctx_in = sb(att, "ctx_in", [P, KT, T])
        bq = sb(att, "bq", [P, KT])
        bk = sb(att, "bk", [P, KT])
        bv = sb(att, "bv", [P, NG])
        bo = sb(att, "bo", [P, H])
        gamma = sb(att, "gamma", [P, H])
        beta = sb(att, "beta", [P, H])
        mask = sb(att, "mask", [TP, TT, B], i32)
        prob_cap = sb(att, "prob_cap", [TP, TT, B])

        pre = ExitStack()
        stage = [sb(pre, f"stage{i}", [P, KT, H]) for i in range(2)]
        wq = [sb(pre, f"wq{i}", [P, KT, H], fp32r) for i in range(2)]
        xq = [sb(pre, f"xq{i}", [S, CB, H]) for i in range(2)]
        qstats = sb(pre, "qstats", [S, CB, 6])
        qmv = sb(pre, "qmv", [S, CB, 2])
        qvar = sb(pre, "qvar", [S, CB])
        qrstd = sb(pre, "qrstd", [S, CB])
        hs = sb(pre, "hs", [S, CB, H])
        hs_t = [[sb(pre, f"hs_t{s}{i}", [P, KT, CH], fp32r) for i in range(2)] for s in range(2)]
        qneg = sb(pre, "qneg", [S, CB])
        bv_p = [sb(pre, f"bv_p{i}", [P, KT, S], fp32r) for i in range(2)]
        q_out = sb(pre, "q_out", [P, 2, 2, CH], fp32r)

        ctx_loaded = sem("ctx_loaded")
        zeroed = sem("zeroed")
        ctx_hi = sem("ctx_hi")
        ctx_lo = sem("ctx_lo")
        xf_loaded = sem("xf_loaded")
        gate_mm = sem("gate_mm")
        up_mm = sem("up_mm")
        wf_loaded = [sem(f"wf_loaded{j}") for j in range(JT - LATE)]
        c_const = sem("c_const")
        c_w = [sem(f"c_w{i}") for i in range(2)]
        c_x = [sem(f"c_x{i}") for i in range(2)]
        c_ident = sem("c_ident")
        neg_half_set = sem("neg_half_set")
        tanh_done = sem("tanh_done")
        consts_done = sem("consts_done")
        cap_done = sem("cap_done")
        wsplit_hi = sem("wsplit_hi")
        w_lo_pool = sem("w_lo_pool")
        bv_split = sem("bv_split")
        bo_mm = sem("bo_mm")
        q_stats = sem("q_stats")
        q_rstd = sem("q_rstd")
        q_pool = sem("q_pool")
        hs_done = sem("hs_done")
        hs_tr = sem("hs_tr")
        hs_hi = sem("hs_hi")
        hs_lo = sem("hs_lo")
        q_mm = sem("q_mm")
        q_hi = sem("q_hi")
        q_lo = sem("q_lo")
        q_stored = [sem(f"q_stored{i}") for i in range(2)]
        bits_done = sem("bits_done")
        masks_done = sem("masks_done")
        pair_done = sem("pair_done")
        picked = sem("picked")
        w_hi_done = sem("w_hi_done")
        w_lo_done = sem("w_lo_done")
        w_stored = [sem(f"w_stored{i}") for i in range(2)]

        def lookup_masks(dve, b):
            need(dve, pair_done, NPAIR * LB * b)
            low = idx[:].bitcast(u16)[:, 0:2 * LW:2]
            nc.vector.tensor_scalar(bit0[:], low, 1, None, ALU.bitwise_and).then_inc(bits_done, 1)
            nc.vector.tensor_scalar(pair_id[:], low, MASK_BITS, None, ALU.bitwise_and).then_inc(bits_done, 1)
            need(dve, picked, PICKS * LB * b)
            dve.wait_ge(bits_done, 2 * b + 2)
            for j in range(1, NPAIR):
                nc.vector.tensor_scalar(pair_mask[:, j - 1, :], pair_id[:], float(2 * j), None, ALU.is_equal)\
                    .then_inc(masks_done, 1)

        def lookup_pair(act, b, k, j):
            n = LB * b + k
            part = slice(k * LP, (k + 1) * LP)
            if j == 0:
                act.wait_ge(bits_done, 2 * b + 1)
                need(act, w_lo_done, n - 1)
                out = w_val[k][:]
            else:
                need(act, picked, PICKS * n + j - 2)
                out = pair_ps[(k + j) % 2][:, 0:LP]
            nc.scalar.activation(out, bit0[:, part], ACT.Identity, scale=lut_step[:, j:j + 1],
                                 bias=lut[:, 2 * j:2 * j + 1]).then_inc(pair_done, 1)

        def lookup_pick(dve, b, k, j):
            n = LB * b + k
            if j == 1 and k == 0:
                dve.wait_ge(masks_done, PICKS * (b + 1))
            if j > 1:
                dve.wait_ge(picked, PICKS * n + j - 1)
            need_apart(dve, pair_done, NPAIR * n + j + 1)
            nc.vector.copy_predicated(w_val[k][:], pair_mask[:, j - 1, k * LP:(k + 1) * LP],
                                      pair_ps[(k + j) % 2][:, 0:LP]).then_inc(picked, 1)

        def lookup_hi(act, b, k):
            act.wait_ge(picked, PICKS * (LB * b + k + 1))
            need(act, w_stored[k], 32 * b)
            nc.scalar.activation(w_hi[k][:], w_val[k][:], ACT.Copy).then_inc(w_hi_done, 1)

        def lookup_lo(pool, b, k):
            pool.wait_ge(w_hi_done, LB * b + k + 1)
            nc.gpsimd.tensor_tensor(w_lo[k][:], w_val[k][:], w_hi[k][:], ALU.subtract).then_inc(w_lo_done, 1)

        def lookup_store(sp, b, k):
            sp.wait_ge(w_lo_done, LB * b + k + 1)
            for a, part in enumerate((w_hi[k], w_lo[k])):
                sp.dma_start(w_dram[:, a, bass.ds(b * LW + k * LP, LP)], part[:].bitcast(fp32))\
                    .then_inc(w_stored[k], 16)

        N_CONST = 11
        hs_banks = score_ps + pv_ps
        with nc.Block() as block:
            @block.sync
            def _(sp):
                sp.dma_start(xq[0][:], ins["x4"][0]).then_inc(c_x[0], 16)
                sp.dma_start(stage[0][:], ins["wq"]).then_inc(c_w[0], 16)
                sp.dma_start(xq[1][:], ins["x4"][1]).then_inc(c_x[1], 16)
                for tile, name in ((bq, "bq"), (bk, "bk"), (bv, "bv"), (bo, "bo"), (gamma, "gamma"), (beta, "beta"),
                                   (lut, "lut")):
                    sp.dma_start(tile[:], ins[name]).then_inc(c_const, 16)
                sp.dma_start(gates[:, 0:1], ins["g_xattn"]).then_inc(c_const, 16)
                sp.dma_start(gates[:, 1:2], ins["g_ffn"]).then_inc(c_const, 16)
                sp.dma_start(res[:, 0:1], ins["res"]).then_inc(c_const, 16)
                sp.dma_start(mask[:], ins["mask"]).then_inc(c_const, 16)
                sp.dma_start(stage[1][:], ins["wk"]).then_inc(c_w[1], 16)
                sp.wait_ge(w_lo_pool, 1)
                sp.dma_start(stage[0][:], ins["wv"]).then_inc(c_w[0], 16)
                sp.wait_ge(hs_done, CB)
                sp.dma_start(xq[0][:], ins["x4"][2]).then_inc(c_x[0], 16)
                sp.dma_start(ctx_in[:], ins["ctx"][0]).then_inc(ctx_loaded, 16)
                for c in range(NC):
                    for m in range(KT):
                        sp.wait_ge(q_lo, KT * c + m + 1)
                        sp.dma_start(q_dram[:, :, m, bass.ds(c * CH, CH)], q_out[:, m % 2, :, :].bitcast(fp32))\
                            .then_inc(q_stored[m % 2], 16)
                        if m == 2 and c == 0:
                            sp.wait_ge(w_lo_pool, 2)
                            sp.dma_start(stage[1][:], ins["wo"]).then_inc(c_w[1], 16)
                        if m == 3 and c == 0:
                            sp.wait_ge(hs_done, 2 * CB)
                            sp.dma_start(xq[1][:], ins["x4"][3]).then_inc(c_x[1], 16)
                for i in range(2):
                    sp.wait_ge(q_stored[i], 16 * NC * KT // 2)

            @block.gpsimd
            def _(pool):
                nc.gpsimd.memset(ident[:], 0.0).then_inc(c_ident, 1)
                nc.gpsimd.memset(neg_half[:], -0.5).then_inc(neg_half_set, 1)
                pool.wait_ge(c_ident, 1)
                nc.gpsimd.affine_select(out=ident[:], in_=ident[:], compare_op=ALU.not_equal, fill=1.0, base=0,
                                        pattern=[[-1, P]], channel_multiplier=1).then_inc(c_ident, 1)
                pool.wait_ge(neg_half_set, 1)

                def normalise(c):
                    pool.wait_ge(q_stats, 2 * CB * (c + 1))
                    nc.gpsimd.tensor_scalar(qvar[:], qmv[:, :, 1], EPS_LN, 1.0, ALU.add, ALU.mult).then_inc(q_pool, 1)
                    nc.gpsimd.tensor_scalar(qneg[:], qmv[:, :, 0], -1.0, 0.0, ALU.mult, ALU.add).then_inc(q_pool, 1)
                    pool.wait_ge(q_pool, 2 * (c + 1))
                    nc.gpsimd.tensor_tensor(qrstd[:], qvar[:], neg_half[0:S, :], ALU.pow).then_inc(q_rstd, 1)
                    if c == 0:
                        return
                    pool.wait_ge(q_rstd, c + 1)
                    pool.wait_ge(hs_tr, KT * c)
                    for i in range(CB):
                        nc.gpsimd.tensor_scalar(hs[:, i, :], xq[c % 2][:, i, :], qneg[:, i:i + 1], qrstd[:, i:i + 1],
                                                ALU.add, ALU.mult).then_inc(hs_done, 1)

                def split_lo(i, dst):
                    pool.wait_ge(wsplit_hi, i + 1)
                    nc.gpsimd.tensor_tensor(dst[1][:], stage[i % 2][:], dst[0][:], ALU.subtract).then_inc(w_lo_pool, 1)
                normalise(0)
                split_lo(0, wq)
                normalise(1)
                split_lo(1, wk)
                normalise(2)
                split_lo(2, wv)
                normalise(3)
                split_lo(3, wo)
                pool.wait_ge(ctx_hi, 1)
                nc.gpsimd.tensor_tensor(ctx_t[0][1][:, :, 0:T], ctx_in[:], ctx_t[0][0][:, :, 0:T], ALU.subtract)\
                    .then_inc(ctx_lo, 1)

            @block.scalar
            def _(act):
                def split_hi(i, dst):
                    act.wait_ge(c_w[i % 2], 16 * (i // 2 + 1))
                    nc.scalar.activation(dst[0][:], stage[i % 2][:], ACT.Copy).then_inc(wsplit_hi, 1)

                def hs_high(c):
                    for k in range(KT):
                        act.wait_ge(hs_tr, KT * c + k + 1)
                        if k == 0:
                            need(act, q_mm, KT * (c - 1))
                        nc.scalar.activation(hs_t[c % 2][0][:, k, :], hs_banks[k][:, 0:CH], ACT.Copy).then_inc(hs_hi, 1)

                split_hi(0, wq)
                act.wait_ge(c_const, 16 * N_CONST)
                nc.scalar.activation(tanh_g[:], gates[:], ACT.Tanh).then_inc(tanh_done, 1)
                nc.scalar.activation(bv_p[0][:], bv[:].unsqueeze(2).broadcast_to([P, KT, S]), ACT.Copy).then_inc(bv_split, 1)
                hs_high(0)
                split_hi(1, wk)
                for c in range(NC):
                    for m in range(KT):
                        if m == KT - 1 and c + 1 < NC:
                            hs_high(c + 1)
                        act.wait_ge(q_mm, KT * c + m + 1)
                        need(act, q_stored[m % 2], 16 * ((KT * c + m) // 2))
                        nc.scalar.activation(q_out[:, m % 2, 0, :], work[m % 2][:, 0:CH], ACT.Identity,
                                             bias=bq[:, m:m + 1]).then_inc(q_hi, 1)
                    if c < 2:
                        split_hi(c + 2, (wv, wo)[c])
                    if c == 2:
                        act.wait_ge(ctx_loaded, 16)
                        nc.scalar.activation(ctx_t[0][0][:, :, 0:T], ctx_in[:], ACT.Copy).then_inc(ctx_hi, 1)

            @block.vector
            def _(dve):
                def stats(c):
                    dve.wait_ge(c_x[c % 2], 16 * (c // 2 + 1))
                    for i in range(CB):
                        nc.vector.bn_stats(qstats[:, i, :], xq[c % 2][:, i, :]).then_inc(q_stats, 1)
                    dve.wait_ge(q_stats, 2 * CB * c + CB)
                    need(dve, hs_done, CB * c)
                    for i in range(CB):
                        nc.vector.bn_aggr(qmv[:, i, :], qstats[:, i, :]).then_inc(q_stats, 1)

                def hs_low(c):
                    for k in range(KT):
                        dve.wait_ge(hs_hi, KT * c + k + 1)
                        nc.vector.tensor_tensor(hs_t[c % 2][1][:, k, :], hs_banks[k][:, 0:CH], hs_t[c % 2][0][:, k, :],
                                                ALU.subtract).then_inc(hs_lo, 1)

                for s in range(2):
                    for i in range(2):
                        nc.vector.memset(ctx_t[s][i][:, :, T:TE].bitcast(fp32), 0.0).then_inc(zeroed, 1)
                stats(0)
                dve.wait_ge(q_rstd, 1)
                for i in range(CB):
                    nc.vector.tensor_scalar(hs[:, i, :], xq[0][:, i, :], qmv[:, i, 0:1], qrstd[:, i:i + 1],
                                            ALU.subtract, ALU.mult).then_inc(hs_done, 1)
                hs_low(0)
                stats(1)
                dve.wait_ge(c_const, 16 * N_CONST)
                nc.vector.tensor_tensor(lut_step[:], lut[:, 1:LUT:2], lut[:, 0:LUT:2], ALU.subtract).then_inc(consts_done, 1)
                nc.vector.tensor_scalar(res[:, 0:1], res[:, 0:1], 0.0, RES_MAX, ALU.max, ALU.min).then_inc(cap_done, 1)
                dve.wait_ge(tanh_done, 1)
                nc.vector.tensor_scalar(gamma[:], gamma[:], tanh_g[:, 0:1], None, ALU.mult).then_inc(cap_done, 1)
                nc.vector.tensor_scalar(beta[:], beta[:], tanh_g[:, 0:1], None, ALU.mult).then_inc(cap_done, 1)
                dve.wait_ge(cap_done, 1)
                nc.vector.tensor_tensor(res[:, 1:2], res[:, 0:1], res[:, 0:1], ALU.mult).then_inc(cap_done, 1)
                nc.vector.tensor_scalar(prob_cap[:], mask[:], 0.5, CLIP_HI, ALU.is_gt, ALU.mult).then_inc(cap_done, 1)
                dve.wait_ge(cap_done, 5)
                nc.vector.tensor_scalar(prob_cap[:], prob_cap[:], CLIP_LO, None, ALU.max).then_inc(cap_done, 1)
                dve.wait_ge(bv_split, 1)
                nc.vector.tensor_tensor(bv_p[1][:], bv[:].unsqueeze(2).broadcast_to([P, KT, S]), bv_p[0][:], ALU.subtract)\
                    .then_inc(bv_split, 1)
                for c in range(NC):
                    for m in range(KT):
                        if m == KT - 1 and c + 1 < NC:
                            hs_low(c + 1)
                        dve.wait_ge(q_hi, KT * c + m + 1)
                        nc.vector.scalar_tensor_tensor(q_out[:, m % 2, 1, :], work[m % 2][:, 0:CH], bq[:, m:m + 1],
                                                       q_out[:, m % 2, 0, :], ALU.add, ALU.subtract).then_inc(q_lo, 1)
                    if c + 2 < NC:
                        stats(c + 2)
                dve.wait_ge(bo_mm, 1)
                nc.vector.tensor_tensor(bo[0:S, :], work[0][0:S, :], bo[0:S, :], ALU.add).then_inc(cap_done, 1)

            @block.tensor
            def _(pe):
                def transposes(c):
                    pe.wait_ge(hs_done, CB * (c + 1))
                    need(pe, hs_lo, KT * c)
                    for k in range(KT):
                        for i in range(CB):
                            mm = nc.tensor.transpose(hs_banks[k][:, i * S:(i + 1) * S], hs[:, i, k * P:(k + 1) * P],
                                                     ident[0:S, 0:S])
                        mm.then_inc(hs_tr, 1)
                pe.wait_ge(c_ident, 2)
                transposes(0)
                pe.wait_ge(w_lo_pool, 1)
                for c in range(NC):
                    pe.wait_ge(hs_lo, KT * (c + 1))
                    for m in range(KT):
                        if m == KT - 1 and c + 1 < NC:
                            transposes(c + 1)
                        need(pe, q_lo, KT * c + m - 1)
                        for n, (a, b) in enumerate(((0, 0), (0, 1), (1, 0))):
                            for k in range(KT):
                                mm = nc.tensor.matmul(work[m % 2][:, 0:CH], wq[a][:, k, m * P:(m + 1) * P],
                                                      hs_t[c % 2][b][:, k, :], start=(n == 0 and k == 0),
                                                      stop=(n == 2 and k == KT - 1))
                        mm.then_inc(q_mm, 1)
                pe.wait_ge(w_lo_pool, 4)
                pe.wait_ge(bv_split, 2)
                pe.wait_ge(q_lo, KT * NC - 1)
                for n, (a, b) in enumerate(((0, 0), (0, 1), (1, 0))):
                    for k in range(KT):
                        mm = nc.tensor.matmul(work[0][0:S, :], bv_p[a][:, k, :], wo[b][:, k, :],
                                              start=(n == 0 and k == 0), stop=(n == 2 and k == KT - 1))
                mm.then_inc(bo_mm, 1)
        pre.close()

        idx = sb(att, "idx", [P, LW], i32)
        bit0 = sb(att, "bit0", [P, LW], u16)
        pair_id = sb(att, "pair_id", [P, LW], u16)
        pair_mask = sb(att, "pair_mask", [P, NPAIR - 1, LW], u16)
        w_val = [sb(att, f"w_val{i}", [P, LP]) for i in range(2)]
        w_hi = [sb(att, f"w_hi{i}", [P, LP], fp32r) for i in range(2)]
        w_lo = [sb(att, f"w_lo{i}", [P, LP], fp32r) for i in range(2)]
        k_t = [[sb(att, f"k_t{s}{i}", [P, NG, TE], fp32r) for i in range(2)] for s in range(2)]
        val = [sb(att, f"val{s}", [TP, TT, NH // 2, 3, HD]) for s in range(2)]
        q_blk = sb(att, "q_blk", [P, 2, NG, GC], fp32r)
        prob = [sb(att, f"prob{s}", [TP, TT, GC]) for s in range(2)]
        den = [sb(att, f"den{s}", [P, 2, S]) for s in range(2)]
        att_t = sb(att, "att_t", [P, NG, S])
        att_p = [sb(att, f"att_p{i}", [P, NG, S], fp32r) for i in range(2)]
        xr = [sb(att, f"xr{s}", [S, H]) for s in range(2)]
        delta = sb(att, "delta", [S, H])
        x1 = sb(att, "x1", [S, H])
        xn = delta
        stats_b = sb(att, "stats_b", [S, 2, 6])
        mv = sb(att, "mv", [S, 2, 2])
        rs_b = sb(att, "rs_b", [S, 6])

        q_loaded = sem("q_loaded")
        x_loaded = [sem(f"x_loaded{i}") for i in range(2)]
        idx_loaded = sem("idx_loaded")
        k_mm = sem("k_mm")
        k_hi = sem("k_hi")
        k_lo = sem("k_lo")
        v_mm = sem("v_mm")
        v_copied = sem("v_copied")
        scores_done = sem("scores_done")
        exp_done = sem("exp_done")
        clip_done = sem("clip_done")
        pv_done = sem("pv_done")
        den_done = sem("den_done")
        divided = sem("divided")
        att_hi = sem("att_hi")
        att_lo = sem("att_lo")
        o_mm = sem("o_mm")
        ln_dve = sem("ln_dve")
        ln_pool = sem("ln_pool")
        xb_done = sem("xb_done")
        xn_tr = sem("xn_tr")
        xn_hi = sem("xn_hi")
        xn_lo = sem("xn_lo")
        x1_tr = sem("x1_tr")
        x1_copied = sem("x1_copied")
        rows_stored = sem("rows_stored")
        inverted = sem("inverted")
        silu_ready = sem("silu_ready")

        def by_pair(half, row, u):
            return pv_ps[half][row:row + HD, 0:4 * S].rearrange("p (g u s) -> p g u s", g=2, u=2)[:, :, u, :]

        gate_ps, up_ps = score_ps, pair_ps

        def wf_cols(a, at, end):
            if end <= 2 * TILE:
                return w_early[at // TILE][a][:, at % TILE:(end - 1) % TILE + 1]
            return wf[a][:, at - 2 * TILE:end - 2 * TILE]

        def gate_w(a, j, k):
            return wf_cols(a, JCOL[j] + k * JW[j], JCOL[j] + (k + 1) * JW[j])

        def up_w(a, j, k):
            return wf_cols(a, JCOL[j] + (KT + k) * JW[j], JCOL[j] + (KT + k + 1) * JW[j])

        def down_w(a, j, m):
            at = JCOL[j] + 2 * KT * JW[j] + m * P
            return wf_cols(a, at, at + P)[0:JW[j], :]

        PARTS = ((0, 0), (0, 1), (1, 0))

        def products(bank, wts, j, slot, n_of):
            for n, (a, b) in enumerate(PARTS):
                for k in range(KT):
                    rows = xf[:, slot, b, k, :] if isinstance(slot, int) else xf[:, bass.ds(slot, 1), b, k, :]
                    mm = nc.tensor.matmul(bank[j % 2][0:JW[j], 0:CH], wts(a, j, k), rows,
                                          start=(n == 0 and k == 0), stop=(n == 2 and k == KT - 1))
            mm.then_inc(n_of, 1)

        LN = 7
        LNP = 7

        def live(b):
            return not isinstance(b, int) or 0 <= b < B

        def is_last(b):
            return isinstance(b, int) and b == B - 1

        def out_bank(b):
            return work[0] if is_last(b) else work[1]

        def value_bank(n, t):
            return work[t % 2] if isinstance(n, int) and n == 0 else work[0]

        def times_gamma(engine, ops, b):
            engine.wait_ge(ln_dve, LN * b + 4)
            ops.tensor_tensor(delta[:], delta[:], gamma[0:S, :], ALU.mult).then_inc(ln_pool, 1)

        def add_x(engine, ops, b, s):
            engine.wait_ge(ln_pool, LNP * b + 4)
            engine.wait_ge(xb_done, b + 1)
            need(engine, x1_tr, b)
            ops.tensor_tensor(x1[:], delta[:], xr[s][:], ALU.add).then_inc(ln_pool, 1)

        def all_iterations(engine, iteration):
            for b in range(-1, 3):
                iteration(b, b % 2)
            with engine.Fori(3, B - 4, 2) as i:
                iteration(i, 1)
                iteration(i + 1, 0)
            for b in range(B - 3, B + 2):
                iteration(b, b % 2)

        with nc.Block() as block:
            @block.tensor
            def _(pe):
                def parts(out, left, right, n_of):
                    todo = [(a, b, k) for a, b in ((0, 0), (0, 1), (1, 0)) for k in range(KT)]
                    for n, (a, b, k) in enumerate(todo):
                        mm = nc.tensor.matmul(out, left(a, k), right(b, k), start=(n == 0), stop=(n == len(todo) - 1))
                        if n == len(todo) // 2 - 1:
                            yield mm
                    mm.then_inc(n_of, 1)
                    yield mm

                def k_unit(n, s, m):
                    if m == 0:
                        pe.wait_ge(ctx_lo, n + 1)
                        if isinstance(n, int) and n == 0:
                            pe.wait_ge(zeroed, 4)
                        if isinstance(n, int) and n < 3:
                            need(pe, k_lo, NG * (n - 1) + 3)
                            if n == 1:
                                pe.wait_ge(v_copied, 2)
                        else:
                            pe.wait_ge(ln_dve, LN * (n - 3) + 1)
                    elif m == 1:
                        need(pe, v_copied, TT * n)
                    else:
                        pe.wait_ge(k_lo, NG * n + m - 1)
                    bank = work[(m + 1) % 2]
                    return parts(bank[:, 0:TE], lambda a, k: wk[a][:, k, m * P:(m + 1) * P],
                                 lambda b, k: ctx_t[s][b][:, k, :], k_mm)

                def v_unit(n, s, t):
                    if isinstance(n, int) and n == 0:
                        if t < 2:
                            pe.wait_ge(k_lo, NG - t)
                        else:
                            pe.wait_ge(v_copied, 1)
                    elif t == 0:
                        pe.wait_ge(k_lo, NG * n + 4)
                    else:
                        pe.wait_ge(v_copied, TT * n + t)
                    return parts(value_bank(n, t)[0:TP, :], lambda a, k: ctx_t[s][a][:, k, t * TP:(t + 1) * TP],
                                 lambda b, k: wv[b][:, k, :], v_mm)

                def out_proj(b):
                    pe.wait_ge(att_lo, b + 1)
                    if is_last(b):
                        pe.wait_ge(v_copied, TT * B)
                    elif isinstance(b, int) and b == 0:
                        pe.wait_ge(k_lo, NG * 2 + 3)
                    else:
                        pe.wait_ge(x1_copied, b)
                    for _ in parts(out_bank(b)[0:S, :], lambda a, k: att_p[a][:, k, :], lambda c, k: wo[c][:, k, :], o_mm):
                        pass

                def transposed(src, done):
                    for k in range(KT):
                        mm = nc.tensor.transpose(work[1][:, k * S:(k + 1) * S], src[:, k * P:(k + 1) * P],
                                                 ident[0:S, 0:S])
                    mm.then_inc(done, 1)

                def transpose_xn(b):
                    pe.wait_ge(ln_dve, LN * (b + 1))
                    if live(b + 3):
                        pe.wait_ge(k_lo, NG * (b + 3) + 3)
                    if is_last(b):
                        pe.wait_ge(x1_copied, b)
                    transposed(xn, xn_tr)

                def transpose_x1(b):
                    pe.wait_ge(xn_lo, b + 1)
                    transposed(x1, x1_tr)

                def scores(b, s, g, t):
                    i = TT * g + t
                    if i == 0:
                        pe.wait_ge(q_loaded, 64 * (b + 1))
                    if t == 0:
                        pe.wait_ge(k_lo, NG * b + g + 1)
                    need(pe, exp_done, TT * NG * b + i - 1)
                    for n, (a, c) in enumerate(((0, 0), (0, 1), (1, 0))):
                        mm = nc.tensor.matmul(score_ps[i % 2][0:TP, 0:GC], k_t[s][a][:, g, t * TP:(t + 1) * TP],
                                              q_blk[:, c, g, :], start=(n == 0), stop=(n == 2))
                    mm.then_inc(scores_done, 1)

                def pv(b, s, g):
                    pe.wait_ge(clip_done, TT * (NG * b + g + 1))
                    if g == 0:
                        pe.wait_ge(v_copied, TT * (b + 1))
                    if g % 2 == 0:
                        need(pe, divided, 4 * (2 * b + g // 2 - 1))
                    for u in range(2):
                        for t in range(TT):
                            for odd in range(2):
                                j = 2 * u + odd
                                h = HG * g + j
                                col = ((g % 2) * 2 + u) * S
                                mm = nc.tensor.matmul(pv_ps[g // 2][64 * odd:64 * odd + 64, col:col + S],
                                                      val[s][:, t, h // 2, odd:odd + 2, :],
                                                      prob[g % 2][:, t, j * S:(j + 1) * S],
                                                      start=(t == 0), stop=(t == TT - 1))
                    mm.then_inc(pv_done, 1)

                def first_products(j):
                    pe.wait_ge(wf_loaded[j], 32)
                    pe.wait_ge(exp_done, TT * NG * B)
                    products(gate_ps, gate_w, j, 0, gate_mm)
                    pe.wait_ge(picked, PICKS * LB * B)
                    products(up_ps, up_w, j, 0, up_mm)

                def iteration(b, s):
                    def project():
                        if live(b + 1):
                            for m in range(NG):
                                yield from k_unit(b + 1, 1 - s, m)
                            for t in range(TT):
                                yield from v_unit(b + 1, 1 - s, t)
                    halves = project()

                    def half():
                        next(halves, None)

                    def sc(g, t):
                        if live(b):
                            scores(b, s, g, t)

                    def out(g):
                        if live(b):
                            pv(b, s, g)
                    if is_last(b - 1):
                        pe.wait_ge(xf_loaded, 16)
                        first_products(0)
                        out_proj(b - 1)
                    sc(0, 0); half(); sc(0, 1); half(); sc(0, 2); half()
                    sc(1, 0); half(); sc(1, 1); half(); sc(1, 2)
                    out(0); half()
                    sc(2, 0); half(); sc(2, 1); half(); sc(2, 2)
                    out(1)
                    if live(b - 2):
                        transpose_xn(b - 2)
                    half(); sc(3, 0); half(); sc(3, 1); sc(3, 2)
                    if live(b - 2):
                        transpose_x1(b - 2)
                    if is_last(b - 1):
                        first_products(1)
                    half(); out(2); half()
                    if live(b - 1) and not is_last(b - 1):
                        out_proj(b - 1)
                    half(); out(3); half()

                all_iterations(pe, iteration)

            @block.scalar
            def _(act):
                def split_ctx(n, s):
                    act.wait_ge(ctx_loaded, 16 * (n + 1))
                    need(act, v_mm, TT * (n - 1))
                    nc.scalar.activation(ctx_t[s][0][:, :, 0:T], ctx_in[:], ACT.Copy).then_inc(ctx_hi, 1)

                def key_hi(n, s, m):
                    act.wait_ge(k_mm, NG * n + m + 1)
                    if m == 0:
                        need(act, scores_done, TT * NG * (n - 1))
                    nc.scalar.activation(k_t[s][0][:, m, :], work[(m + 1) % 2][:, 0:TE], ACT.Identity,
                                         bias=bk[:, m:m + 1]).then_inc(k_hi, 1)

                def value(n, s, t):
                    act.wait_ge(v_mm, TT * n + t + 1)
                    if t == 0:
                        need(act, pv_done, NG * (n - 1))
                        if isinstance(n, int) and n < 2:
                            act.wait_ge(zeroed, 6)
                    nc.scalar.activation(val[s][:, t, :, 0:3:2, :], value_bank(n, t)[0:TP, :].rearrange(
                        "p (h o d) -> p h o d", o=2, d=HD), ACT.Copy).then_inc(v_copied, 1)

                def exp(b, g, t):
                    i = TT * g + t
                    act.wait_ge(scores_done, TT * NG * b + i + 1)
                    if t == 0:
                        need(act, pv_done, NG * b + g - 1)
                    nc.scalar.activation(prob[g % 2][:, t, :], score_ps[i % 2][0:TP, 0:GC], ACT.Exp,
                                         scale=SCORE_SCALE).then_inc(exp_done, 1)

                def sums(b, half):
                    act.wait_ge(pv_done, NG * b + 2 * half + 2)
                    need(act, divided, 4 * (2 * b + half - 1))
                    for odd in range(2):
                        for u in range(2):
                            q = HD * (2 * odd + u)
                            nc.scalar.activation(den[half][q:q + HD, :, :], by_pair(half, 32 + 32 * odd, u), ACT.Copy,
                                                 scale=1.0 + EPS_PROBS).then_inc(den_done, 1)

                def att_high(b):
                    act.wait_ge(divided, 8 * (b + 1))
                    need(act, o_mm, b)
                    nc.scalar.activation(att_p[0][:], att_t[:], ACT.Copy).then_inc(att_hi, 1)

                def xn_high(b):
                    act.wait_ge(xn_tr, b + 1)
                    need(act, rows_stored, 32 * b)
                    nc.scalar.activation(xn_p[:, 0, :, :], work[1][:, 0:KT * S].rearrange("p (k s) -> p k s", k=KT),
                                         ACT.Copy).then_inc(xn_hi, 1)

                def x1_copy(b):
                    act.wait_ge(x1_tr, b + 1)
                    nc.scalar.activation(x1_t[:], work[1][:, 0:KT * S].rearrange("p (k s) -> p k s", k=KT),
                                         ACT.Copy).then_inc(x1_copied, 1)

                def iteration(b, s):
                    steps = iter([(k, j) for k in range(LB) for j in range(NPAIR)])

                    def ex(g, t):
                        if live(b):
                            exp(b, g, t)

                    def look():
                        if live(b):
                            lookup_pair(act, b, *next(steps))

                    def kh(m):
                        if live(b + 1):
                            key_hi(b + 1, 1 - s, m)

                    def va(t):
                        if live(b + 1):
                            value(b + 1, 1 - s, t)
                    ex(0, 0); look(); ex(0, 1)
                    if is_last(b - 1):
                        sums(b - 1, 1)
                    if live(b - 1):
                        lookup_hi(act, b - 1, 1)
                    kh(0); ex(0, 2); look()
                    if live(b - 1) and not is_last(b - 1):
                        sums(b - 1, 1)
                    ex(1, 0); kh(1); look(); ex(1, 1); look(); ex(1, 2)
                    if live(b - 1):
                        att_high(b - 1)
                    kh(2); look(); ex(2, 0); look(); ex(2, 1); kh(3); look(); ex(2, 2)
                    if live(b):
                        sums(b, 0)
                    if live(b - 2):
                        xn_high(b - 2)
                    look(); ex(3, 0); look(); va(0); ex(3, 1); look(); ex(3, 2)
                    if live(b + 2):
                        split_ctx(b + 2, s)
                    look()
                    if live(b - 2):
                        x1_copy(b - 2)
                    look(); va(1)
                    if live(b):
                        lookup_hi(act, b, 0)
                    look(); look(); look(); look(); va(2)
                    if is_last(b - 1):
                        nc.scalar.activation(gates[:], gates[:], ACT.Silu).then_inc(silu_ready, 1)

                all_iterations(act, iteration)

            @block.vector
            def _(dve):
                for s in range(2):
                    nc.vector.memset(val[s][:, :, :, 1, :], 1.0).then_inc(zeroed, 1)
                nc.vector.memset(q_blk[:].bitcast(fp32), 0.0).then_inc(zeroed, 1)

                def clip(b, g, t):
                    dve.wait_ge(exp_done, TT * (NG * b + g) + t + 1)
                    p_ = prob[g % 2][:, t, :]
                    nc.vector.tensor_scalar(p_, p_, CLIP_LO, prob_cap[:, t, bass.ds(b, 1)], ALU.max, ALU.min)\
                        .then_inc(clip_done, 1)

                def key_lo(n, s, m):
                    dve.wait_ge(k_hi, NG * n + m + 1)
                    nc.vector.scalar_tensor_tensor(k_t[s][1][:, m, :], work[(m + 1) % 2][:, 0:TE],
                                                   bk[:, m:m + 1], k_t[s][0][:, m, :], ALU.add, ALU.subtract)\
                        .then_inc(k_lo, 1)

                def divide(b, half):
                    dve.wait_ge(den_done, 4 * (2 * b + half + 1))
                    nc.vector.reciprocal(den[half][:], den[half][:]).then_inc(inverted, 1)
                    dve.wait_ge(inverted, 2 * b + half + 1)
                    need(dve, att_lo, b)
                    for odd in range(2):
                        for u in range(2):
                            q = HD * (2 * odd + u)
                            nc.vector.tensor_tensor(att_t[q:q + HD, 2 * half:2 * half + 2, :],
                                                    by_pair(half, 96 * odd, u), den[half][q:q + HD, :, :],
                                                    ALU.mult).then_inc(divided, 1)

                def ln(b, k):
                    done = LN * b
                    if k == 0:
                        dve.wait_ge(o_mm, b + 1)
                        need(dve, xn_tr, b)
                        nc.vector.tensor_tensor(delta[:], out_bank(b)[0:S, :], bo[0:S, :], ALU.add).then_inc(ln_dve, 1)
                    elif k == 1:
                        need_apart(dve, ln_dve, done + 1)
                        nc.vector.bn_stats(stats_b[:, 0, :], delta[:]).then_inc(ln_dve, 1)
                    elif k == 2:
                        need_apart(dve, ln_dve, done + 2)
                        nc.vector.bn_aggr(mv[:, 0, :], stats_b[:, 0, :]).then_inc(ln_dve, 1)
                    elif k == 3:
                        dve.wait_ge(ln_pool, LNP * b + 3)
                        nc.vector.tensor_scalar(delta[:], delta[:], mv[:, 0, 0:1], rs_b[:, 2:3], ALU.subtract, ALU.mult)\
                            .then_inc(ln_dve, 1)
                    elif k == 4:
                        need_apart(dve, ln_pool, LNP * b + 5)
                        nc.vector.bn_stats(stats_b[:, 1, :], x1[:]).then_inc(ln_dve, 1)
                    elif k == 5:
                        need_apart(dve, ln_dve, done + 5)
                        nc.vector.bn_aggr(mv[:, 1, :], stats_b[:, 1, :]).then_inc(ln_dve, 1)
                    else:
                        dve.wait_ge(ln_pool, LNP * b + 7)
                        need(dve, xn_tr, b)
                        nc.vector.tensor_scalar(xn[:], x1[:], mv[:, 1, 0:1], rs_b[:, 4:5], ALU.subtract, ALU.mult)\
                            .then_inc(ln_dve, 1)

                def xn_low(b):
                    dve.wait_ge(xn_hi, b + 1)
                    nc.vector.tensor_tensor(xn_p[:, 1, :, :], work[1][:, 0:KT * S].rearrange("p (k s) -> p k s", k=KT),
                                            xn_p[:, 0, :, :], ALU.subtract).then_inc(xn_lo, 1)

                def iteration(b, s):
                    steps = iter([(k, j) for k in range(LB) for j in range(1, NPAIR)])

                    def cl(g, t):
                        if live(b):
                            clip(b, g, t)

                    def kl(m):
                        if live(b + 1):
                            key_lo(b + 1, 1 - s, m)

                    def look():
                        if live(b):
                            lookup_pick(dve, b, *next(steps))

                    def lns(b, *ks):
                        if live(b):
                            for k in ks:
                                ln(b, k)
                    cl(0, 0); lns(b - 2, 3)
                    if is_last(b - 2):
                        times_gamma(dve, nc.vector, b - 2)
                        add_x(dve, nc.vector, b - 2, s)
                    cl(0, 1); kl(0); cl(0, 2); look()
                    if live(b - 1):
                        divide(b - 1, 1)
                    if is_last(b - 1):
                        dve.wait_ge(att_hi, B)
                        nc.vector.tensor_tensor(att_p[1][:], att_t[:], att_p[0][:], ALU.subtract).then_inc(att_lo, 1)
                    cl(1, 0); kl(1); look(); cl(1, 1); look(); cl(1, 2); lns(b - 2, 4)
                    kl(2); look(); lns(b - 2, 5); cl(2, 0); look(); cl(2, 1); kl(3); lns(b - 2, 6); look(); cl(2, 2)
                    if live(b):
                        divide(b, 0)
                    cl(3, 0)
                    if live(b - 2):
                        xn_low(b - 2)
                    look(); cl(3, 1); look(); cl(3, 2); look(); look()
                    lns(b - 1, 0); look(); lns(b - 1, 1); look(); lns(b - 1, 2); look(); look()
                    if live(b + 1):
                        next_masks(b + 1)

                def next_masks(b):
                    dve.wait_ge(idx_loaded, 16 * (b + 1))
                    lookup_masks(dve, b)

                all_iterations(dve, iteration)

            @block.gpsimd
            def _(pool):
                def split_ctx(n, s):
                    pool.wait_ge(ctx_hi, n + 1)
                    nc.gpsimd.tensor_tensor(ctx_t[s][1][:, :, 0:T], ctx_in[:], ctx_t[s][0][:, :, 0:T], ALU.subtract)\
                        .then_inc(ctx_lo, 1)

                def add_beta(b, s):
                    pool.wait_ge(x_loaded[s], 16 * ((b + 2 - s) // 2) if isinstance(b, int) else 8 * (b + 2 - s))
                    nc.gpsimd.tensor_tensor(xr[s][:], xr[s][:], beta[0:S, :], ALU.add).then_inc(xb_done, 1)

                def att_low(b):
                    pool.wait_ge(att_hi, b + 1)
                    nc.gpsimd.tensor_tensor(att_p[1][:], att_t[:], att_p[0][:], ALU.subtract).then_inc(att_lo, 1)

                def ln(b, s, k):
                    done = LNP * b
                    if k == 0:
                        need_apart(pool, ln_dve, LN * b + 3)
                        nc.gpsimd.tensor_scalar(rs_b[:, 0:1], mv[:, 0, 1:2], res[0:S, 1:2], EPS_LN, ALU.mult, ALU.add)\
                            .then_inc(ln_pool, 1)
                    elif k == 1:
                        pool.wait_ge(ln_pool, done + 1)
                        nc.gpsimd.tensor_tensor(rs_b[:, 1:2], rs_b[:, 0:1], neg_half[0:S, 0:1], ALU.pow)\
                            .then_inc(ln_pool, 1)
                    elif k == 2:
                        pool.wait_ge(ln_pool, done + 2)
                        nc.gpsimd.tensor_tensor(rs_b[:, 2:3], rs_b[:, 1:2], res[0:S, 0:1], ALU.mult).then_inc(ln_pool, 1)
                    elif k == 3:
                        times_gamma(pool, nc.gpsimd, b)
                    elif k == 4:
                        add_x(pool, nc.gpsimd, b, s)
                    elif k == 5:
                        need_apart(pool, ln_dve, LN * b + 6)
                        nc.gpsimd.tensor_scalar(rs_b[:, 3:4], mv[:, 1, 1:2], EPS_LN, 1.0, ALU.add, ALU.mult)\
                            .then_inc(ln_pool, 1)
                    else:
                        pool.wait_ge(ln_pool, done + 6)
                        nc.gpsimd.tensor_tensor(rs_b[:, 4:5], rs_b[:, 3:4], neg_half[0:S, 0:1], ALU.pow)\
                            .then_inc(ln_pool, 1)

                def iteration(b, s):
                    def lns(b, s, *ks):
                        if live(b):
                            for k in ks:
                                ln(b, s, k)
                    if live(b - 1):
                        lookup_lo(pool, b - 1, 1)
                    if not is_last(b - 2):
                        lns(b - 2, s, 3, 4)
                    if live(b - 1):
                        if not is_last(b - 1):
                            att_low(b - 1)
                        add_beta(b - 1, 1 - s)
                    lns(b - 2, s, 5, 6)
                    if live(b + 2):
                        split_ctx(b + 2, s)
                    if live(b):
                        lookup_lo(pool, b, 0)
                    lns(b - 1, 1 - s, 0, 1, 2)

                all_iterations(pool, iteration)

            @block.sync
            def _(sp):
                def load_ctx(n):
                    need(sp, ctx_lo, n)
                    sp.dma_start(ctx_in[:], ins["ctx"][n]).then_inc(ctx_loaded, 16)

                def load_q(b):
                    need(sp, scores_done, TT * NG * b)
                    for j in range(HG):
                        sp.dma_start(q_blk[j * HD:(j + 1) * HD, :, :, j * S:(j + 1) * S].bitcast(fp32),
                                     q_dram[j * HD:(j + 1) * HD, :, :, bass.ds(b * S, S)]).then_inc(q_loaded, 16)

                def load_x(b, s):
                    need(sp, ln_pool, LNP * (b - 2) + 5)
                    sp.dma_start(xr[s][:], ins["x"][bass.ds(b * S, S), :]).then_inc(x_loaded[s], 16)

                def load_idx(b):
                    need(sp, bits_done, 2 * b)
                    sp.dma_start(idx[:], ins["idx"][:, bass.ds(b * LW, LW)]).then_inc(idx_loaded, 16)

                def early_tile(j, done, count):
                    for k in range(LB):
                        sp.wait_ge(w_stored[k], 32 * (B - 3))
                    sp.wait_ge(done, count)
                    if j == 1:
                        sp.wait_ge(rows_stored, 32 * (B - 4))
                        sp.dma_start(xf[:, 0].rearrange("p a k s -> p (a k) s").bitcast(fp32),
                                     xn_dram[:, :, :, 0:CH].rearrange("p a k s -> p (a k) s")).then_inc(xf_loaded, 16)
                    for a in range(2):
                        sp.dma_start(w_early[j][a].bitcast(fp32), w_dram[:, a, j * TILE:(j + 1) * TILE])\
                            .then_inc(wf_loaded[j], 16)

                def store_rows(b):
                    sp.wait_ge(xn_lo, b + 1)
                    sp.dma_start(xn_dram[:, :, :, bass.ds(b * S, S)].rearrange("p a k s -> p (a k) s"),
                                 xn_p[:].rearrange("p a k s -> p (a k) s").bitcast(fp32)).then_inc(rows_stored, 16)
                    sp.wait_ge(x1_copied, b + 1)
                    sp.dma_start(x1_dram[:, :, bass.ds(b * S, S)], x1_t[:]).then_inc(rows_stored, 16)

                def iteration(b, s):
                    if live(b):
                        load_x(b, s)
                    if live(b - 1):
                        lookup_store(sp, b - 1, 1)
                    if live(b + 1) and live(b):
                        load_idx(b + 1)
                        load_q(b + 1)
                    if is_last(b + 1):
                        early_tile(0, k_mm, NG * B)
                    if is_last(b):
                        early_tile(1, v_mm, TT * B)
                    if live(b - 2):
                        store_rows(b - 2)
                    if live(b):
                        lookup_store(sp, b, 0)
                    if live(b + 3):
                        load_ctx(b + 3)

                load_ctx(1)
                sp.wait_ge(zeroed, 7)
                load_q(0)
                load_idx(0)
                all_iterations(sp, iteration)
                for k in range(LB):
                    sp.wait_ge(w_stored[k], 32 * B)
        att.close()

        ffn = ExitStack()
        wf = [sb(ffn, f"wf{i}", [P, WCOLS - 2 * TILE], fp32r) for i in range(2)]
        x1f = sb(ffn, "x1f", [P, 2, KT, CH])
        idx2 = x1f[:].rearrange("p a k s -> p (a k s)")[:, 0:WCOLS - LATE_COL].bitcast(i32)
        silu = [sb(ffn, f"silu{s}", [P, CH]) for s in range(2)]
        hid = [sb(ffn, f"hid{s}", [P, CH]) for s in range(2)]

        bit0_2 = sb(ffn, "bit0_2", [P, LATE_LP], u16)
        pair_id2 = sb(ffn, "pair_id2", [P, LATE_LP], u16)
        pair_mask2 = sb(ffn, "pair_mask2", [P, NPAIR - 1, LATE_LP], u16)
        pair_val = [sb(ffn, f"pair_val{i}", [P, LATE_LP]) for i in range(2)]
        w_val2 = sb(ffn, "w_val2", [P, LATE_LP])

        x1f_loaded = sem("x1f_loaded")
        silu_done = sem("silu_done")
        late_idx = sem("late_idx")
        late_bits = sem("late_bits")
        late_masks = sem("late_masks")
        late_pair = sem("late_pair")
        late_picked = sem("late_picked")
        late_hi = sem("late_hi")
        late_lo = sem("late_lo")
        hid_done = sem("hid_done")
        hid_hi = sem("hid_hi")
        hid_lo = sem("hid_lo")
        down_mm = sem("down_mm")
        down_all = sem("down_all")
        y_done = sem("y_done")
        y_stored = [sem(f"y_stored{s}") for s in range(2)]
        acc = pv_ps + work
        LATE_RATE = 2, 3
        FREE = 2

        with nc.Block() as block:
            @block.sync
            def _(sp):
                def load_xn(c):
                    sp.wait_ge(xf_loaded, 16 * c)
                    sp.dma_start(xf[:, c % 2].rearrange("p a k s -> p (a k) s").bitcast(fp32),
                                 xn_dram[:, :, :, c * CH:(c + 1) * CH].rearrange("p a k s -> p (a k) s"))\
                        .then_inc(xf_loaded, 16)

                def load_x1(c):
                    need(sp, x1f_loaded, 16 * c)
                    sp.dma_start(x1f[:, c % 2, :, :], x1_dram[:, :, c * CH:(c + 1) * CH]).then_inc(x1f_loaded, 16)
                for j in range(2, JT - LATE):
                    for a in range(2):
                        sp.dma_start(wf_cols(a, JCOL[j], JCOL[j + 1]).bitcast(fp32), w_dram[:, a, JCOL[j]:JCOL[j + 1]])\
                            .then_inc(wf_loaded[j], 16)
                    if j == 2:
                        sp.dma_start(idx2, ins["idx"][:, LATE_COL:WCOLS]).then_inc(late_idx, 16)
                load_xn(1)
                sp.wait_ge(late_bits, 2 * len(LATE_PIECES))
                load_x1(0)
                load_x1(1)
                for c in range(NC):
                    for m in range(KT):
                        sp.wait_ge(y_done, KT * (c + 1) + m + 1)
                        sp.dma_start(out_t[m, :, c * CH:(c + 1) * CH], x1f[:, c % 2, m, :]).then_inc(y_stored[c % 2], 16)
                    if c + 2 < NC:
                        if c + 2 == NC - 1:
                            sp.wait_ge(rows_stored, 32 * B)
                        load_xn(c + 2)
                        sp.wait_ge(y_stored[c % 2], 16 * KT)
                        load_x1(c + 2)
                for s in range(2):
                    sp.wait_ge(y_stored[s], 16 * KT * NC // 2)

            @block.tensor
            def _(pe):
                def up_units(c, slot, j):
                    if j == 0:
                        pe.wait_ge(xf_loaded, 16 * (c + 1))
                    if j < JT - LATE:
                        pe.wait_ge(wf_loaded[j], 32)
                    else:
                        end = JCOL[j + 1] if j + 1 < JT else WCOLS
                        pe.wait_ge(late_lo, -(-(end - LATE_COL) // LATE_LP))
                    pe.wait_ge(silu_done, JT * c + j - (j > 0) + FREE)
                    products(gate_ps, gate_w, j, slot, gate_mm)
                    pe.wait_ge(hid_done, JT * c + j - (j > 0) + FREE)
                    products(up_ps, up_w, j, slot, up_mm)

                def down_units(c, j):
                    pe.wait_ge(hid_lo, JT * c + j + 1 + FREE)
                    if j == 0:
                        pe.wait_ge(y_done, KT * (c + 1))
                    if j == JT - 1:
                        pe.wait_ge(x1f_loaded, 16 * (c + 1))
                    for m in range(KT):
                        for n, (a, b) in enumerate(PARTS):
                            mm = nc.tensor.matmul(acc[m][:, 0:CH], down_w(a, j, m), hid_p[j % 2][b][0:JW[j], :],
                                                  start=(j == 0 and n == 0), stop=(j == JT - 1 and n == 2))
                        if j == JT - 1 and m < KT - 1:
                            mm.then_inc(down_all, 1)
                    mm.then_inc(down_mm, 1)

                pe.sem_inc(down_mm, FREE)
                down_units(0, 0)
                down_units(0, 1)
                up_units(0, 0, 2)
                for j in range(3, JT):
                    up_units(0, 0, j)
                    down_units(0, j - 1)
                down_units(0, JT - 1)
                with pe.Fori(1, NC, 1) as c:
                    up_units(c, c % 2, 0)
                    for j in range(1, JT):
                        up_units(c, c % 2, j)
                        down_units(c, j - 1)
                    down_units(c, JT - 1)

            @block.scalar
            def _(act):
                def silu_of(c, j):
                    w = JW[j]
                    act.wait_ge(gate_mm, JT * c + j + 1)
                    act.wait_ge(hid_done, JT * c + j - (j > 0) + FREE)
                    nc.scalar.activation(silu[j % 2][0:w, :], gate_ps[j % 2][0:w, 0:CH], ACT.Silu).then_inc(silu_done, 1)

                def high_of(c, j):
                    w = JW[j]
                    act.wait_ge(hid_done, JT * c + j + 1 + FREE)
                    act.wait_ge(down_mm, JT * c + j - (j > 0) + FREE)
                    nc.scalar.activation(hid_p[j % 2][0][0:w, :], hid[j % 2][0:w, :], ACT.Copy).then_inc(hid_hi, 1)

                def late_steps():
                    for n, col, width in LATE_PIECES:
                        for j in range(NPAIR):
                            if j == 0:
                                act.wait_ge(late_bits, 2 * n + 1)
                                need(act, late_lo, n)
                                out = w_val2
                            else:
                                need(act, late_picked, PICKS * n + j - 2 - (j == 1))
                                out = pair_val[j % 2]
                            nc.scalar.activation(out[:, 0:width], bit0_2[:, 0:width], ACT.Identity,
                                                 scale=lut_step[:, j:j + 1], bias=lut[:, 2 * j:2 * j + 1])\
                                .then_inc(late_pair, 1)
                            yield
                        act.wait_ge(late_picked, PICKS * (n + 1))
                        nc.scalar.activation(wf_cols(0, col, col + width), w_val2[:, 0:width], ACT.Copy).then_inc(late_hi, 1)
                        yield

                act.sem_inc(silu_done, FREE)
                late = late_steps()
                for j in range(JT):
                    for _ in range(LATE_RATE[0] if j > 1 else 0):
                        next(late, None)
                    silu_of(0, j)
                    for _ in range(LATE_RATE[1] if j > 1 else 0):
                        next(late, None)
                    high_of(0, j)
                with act.Fori(1, NC, 1) as c:
                    for j in range(JT):
                        silu_of(c, j)
                        high_of(c, j)

            @block.vector
            def _(dve):
                def late_steps():
                    for n, col, width in LATE_PIECES:
                        dve.wait_ge(late_idx, 16)
                        need(dve, late_pair, NPAIR * n)
                        at = col - LATE_COL
                        low = idx2.bitcast(u16)[:, 2 * at:2 * (at + width):2]
                        nc.vector.tensor_scalar(bit0_2[:, 0:width], low, 1, None, ALU.bitwise_and).then_inc(late_bits, 1)
                        nc.vector.tensor_scalar(pair_id2[:, 0:width], low, MASK_BITS, None, ALU.bitwise_and)\
                            .then_inc(late_bits, 1)
                        yield
                        dve.wait_ge(late_bits, 2 * n + 2)
                        for j in range(1, NPAIR):
                            nc.vector.tensor_scalar(pair_mask2[:, j - 1, 0:width], pair_id2[:, 0:width], float(2 * j),
                                                    None, ALU.is_equal).then_inc(late_masks, 1)
                        yield
                        dve.wait_ge(late_masks, PICKS * (n + 1))
                        for j in range(1, NPAIR):
                            if j > 1:
                                dve.wait_ge(late_picked, PICKS * n + j - 1)
                            dve.wait_ge(late_pair, NPAIR * n + j + 1)
                            nc.vector.copy_predicated(w_val2[:, 0:width], pair_mask2[:, j - 1, 0:width],
                                                      pair_val[j % 2][:, 0:width]).then_inc(late_picked, 1)
                            yield

                def hidden(c, j):
                    w = JW[j]
                    dve.wait_ge(silu_done, JT * c + j + 1 + FREE)
                    dve.wait_ge(up_mm, JT * c + j + 1)
                    dve.wait_ge(hid_lo, JT * c + j - (j > 0) + FREE)
                    nc.vector.tensor_tensor(hid[j % 2][0:w, :], silu[j % 2][0:w, :], up_ps[j % 2][0:w, 0:CH],
                                            ALU.mult).then_inc(hid_done, 1)

                def hidden_low(c, j):
                    w = JW[j]
                    dve.wait_ge(hid_hi, JT * c + j + 1)
                    nc.vector.tensor_tensor(hid_p[j % 2][1][0:w, :], hid[j % 2][0:w, :], hid_p[j % 2][0][0:w, :],
                                            ALU.subtract).then_inc(hid_lo, 1)

                def output(c, s):
                    for m in range(KT):
                        if m < KT - 1:
                            dve.wait_ge(down_all, (KT - 1) * c + m + 1)
                        else:
                            dve.wait_ge(down_mm, JT * (c + 1) + FREE)
                        nc.vector.scalar_tensor_tensor(x1f[:, s, m, :], acc[m][:, 0:CH], tanh_g[:, 1:2],
                                                       x1f[:, s, m, :], ALU.mult, ALU.add).then_inc(y_done, 1)
                dve.sem_inc(hid_done, FREE)
                dve.sem_inc(hid_lo, FREE)
                dve.sem_inc(y_done, KT)
                late = late_steps()
                for j in range(JT):
                    for _ in range(LATE_RATE[0] if j > 1 else 0):
                        next(late, None)
                    hidden(0, j)
                    for _ in range(LATE_RATE[1] if j > 1 else 0):
                        next(late, None)
                    hidden_low(0, j)
                output(0, 0)
                with dve.Fori(1, NC, 1) as c:
                    for j in range(JT):
                        hidden(c, j)
                        hidden_low(c, j)
                    output(c, c % 2)

            @block.gpsimd
            def _(pool):
                for n, col, width in LATE_PIECES:
                    pool.wait_ge(late_hi, n + 1)
                    nc.gpsimd.tensor_tensor(wf_cols(1, col, col + width), w_val2[:, 0:width],
                                            wf_cols(0, col, col + width), ALU.subtract).then_inc(late_lo, 1)
        ffn.close()


def kernel(**inputs):
    import numpy as np
    import concourse.bacc as bacc
    from concourse import mybir as mb
    from concourse.bass_utils import run_bass_kernel_spmd

    a = {k: np.asarray(v) for k, v in inputs.items()}
    quad = [0, 2, 1, 3]
    order = np.concatenate([np.arange(HD) + HD * (HG * g + quad[q]) for g in range(NG) for q in range(HG)])

    def rows(v):
        return np.ascontiguousarray(np.broadcast_to(v.reshape(1, -1), (P, v.size)))

    def feature_major(w):
        return np.ascontiguousarray(w.T.reshape(KT, P, -1).transpose(1, 0, 2))

    def columns(v):
        return np.ascontiguousarray(v.reshape(KT, P).T)

    gate, up, down = (a["L0_ffn_" + n] for n in ("gate_idx", "up_idx", "down_idx"))
    gate_f, up_f = feature_major(gate), feature_major(up)
    blocks = []
    for j in range(JT):
        cols = slice(j * P, j * P + JW[j])
        blocks += [gate_f[:, :, cols].reshape(P, -1), up_f[:, :, cols].reshape(P, -1)]
        tile = np.zeros((P, H), down.dtype)
        tile[:JW[j]] = down.T[cols]
        blocks.append(tile)
    arrays = {
        "x": np.ascontiguousarray(a["x"].reshape(ROWS, H)),
        "x4": np.ascontiguousarray(a["x"].reshape(NC, CB, S, H).transpose(0, 2, 1, 3)),
        "ctx": np.ascontiguousarray(a["ctx_2048"].reshape(B, T, KT, P).transpose(0, 3, 2, 1)),
        "mask": np.ascontiguousarray(a["mask_BxS2_ik0"].reshape(B, TT, TP).transpose(2, 1, 0)),
        "wq": feature_major(a["L0_xattn_Wq"]),
        "wk": feature_major(a["L0_xattn_Wk"]),
        "wv": feature_major(a["L0_xattn_Wv"]),
        "wo": feature_major(a["L0_xattn_Wo"][:, order]),
        "bq": columns(a["L0_xattn_bq"]),
        "bk": columns(a["L0_xattn_bk"]),
        "bv": columns(a["L0_xattn_bv"][order]),
        "bo": rows(a["L0_xattn_bo"]),
        "gamma": rows(a["L0_xattn_ln_gamma"]),
        "beta": rows(a["L0_xattn_ln_beta"]),
        "lut": rows(a["L0_ffn_lut"]),
        "g_xattn": rows(a["g_xattn"]),
        "g_ffn": rows(a["g_ffn"]),
        "res": rows(a["L0_xattn_residual_scale"].reshape(1)),
        "idx": np.ascontiguousarray(np.concatenate(blocks, axis=1)),
    }
    nc = bacc.Bacc("TRN2", target_bir_lowering=False, num_devices=1)
    ins = {n: nc.dram_tensor(f"in_{n}", v.shape, mb.dt.from_np(v.dtype), kind="ExternalInput").ap()
           for n, v in arrays.items()}
    out_t = nc.dram_tensor("out_t", (KT, P, ROWS), mb.dt.float32, kind="ExternalOutput").ap()
    flamingo_kernel(nc, ins, out_t)
    r = run_bass_kernel_spmd(nc, [{f"in_{n}": v for n, v in arrays.items()}], core_ids=[0])
    got = r.results[0]["out_t"]
    return np.ascontiguousarray(got.reshape(H, ROWS).T).reshape(B, S, H)
```
